# Optimizing a Trainium2 kernel written in Bass

```python
import numpy as np
import jax
import jax.numpy as jnp

def _softmax(x, axis=-1):
    return jax.nn.softmax(x, axis=axis)

def _gelu(x):
    return jax.nn.gelu(x, approximate=True)

def _silu(x):
    return jax.nn.silu(x)

def _sigmoid(x):
    return jax.nn.sigmoid(x)

def _layernorm(x, axis=-1, eps=1e-05):
    m = jnp.mean(x, axis=axis, keepdims=True)
    v = jnp.var(x, axis=axis, keepdims=True)
    return (x - m) / jnp.sqrt(v + eps)

def _scatter_add(tgt, idx, src, axis=0):
    return tgt.at[idx].add(src)

def _segment_sum(src, seg, n):
    return jax.ops.segment_sum(src, seg, n)
kernel_name = 'mk_recurrent_d1_jaxref_r4_7ef1b7'

def setup_inputs(seed: int=0):
    np.random.seed(seed)
    _w = jnp.asarray

    def _L0_attn_setup():
        import jax, jax.numpy as jnp
        import numpy as np
        D_MODEL = 512
        EXPAND = 2
        D_INNER = D_MODEL * EXPAND
        HEAD_DIM = 64
        NHEADS = D_INNER // HEAD_DIM
        D_STATE = 128
        NGROUPS = 1
        D_CONV = 4
        CHUNK = 64
        CONV_DIM = D_INNER + 2 * NGROUPS * D_STATE
        D_IN_PROJ = 2 * D_INNER + 2 * NGROUPS * D_STATE + NHEADS
        EPS = 1e-05

        def segsum(x):
            T = x.shape[-1]
            xc = jnp.cumsum(x, axis=-1)
            diff = xc[..., :, None] - xc[..., None, :]
            mask = jnp.tril(jnp.ones((T, T), dtype=bool))
            return jnp.where(mask, diff, -jnp.inf)

        def causal_conv1d(x, w, b):
            K = w.shape[1]
            L = x.shape[1]
            xp = jnp.pad(x, ((0, 0), (K - 1, 0), (0, 0)))
            y = b[None, None, :]
            for k in range(K):
                y = y + xp[:, k:k + L, :] * w[None, None, :, k]
            return jax.nn.silu(y)

        def ssd_chunked(x, dt, A, B, C, Dskip):
            b, l, h, p = x.shape
            g, n = (B.shape[2], B.shape[3])
            c = l // CHUNK
            xc = x.reshape(b, c, CHUNK, h, p)
            dtc = dt.reshape(b, c, CHUNK, h)
            Bh = jnp.repeat(B.reshape(b, c, CHUNK, g, n), h // g, axis=3)
            Ch = jnp.repeat(C.reshape(b, c, CHUNK, g, n), h // g, axis=3)
            dA = dtc * A[None, None, None, :]
            dAc = jnp.moveaxis(dA, 3, 1)
            A_cumsum = jnp.cumsum(dAc, axis=-1)
            Lmat = jnp.exp(segsum(dAc))
            Y_diag = jnp.einsum('bclhn,bcshn,bhcls,bcsh,bcshp->bclhp', Ch, Bh, Lmat, dtc, xc)
            decay_states = jnp.exp(A_cumsum[..., -1:] - A_cumsum)
            states = jnp.einsum('bclhn,bhcl,bclh,bclhp->bchpn', Bh, decay_states, dtc, xc)
            states = jnp.concatenate([jnp.zeros_like(states[:, :1]), states], axis=1)
            chunk_sums = jnp.pad(A_cumsum[..., -1], ((0, 0), (0, 0), (1, 0)))
            decay_chunk = jnp.exp(segsum(chunk_sums))
            new_states = jnp.einsum('bhzc,bchpn->bzhpn', decay_chunk, states)
            states_prev = new_states[:, :-1]
            state_decay_out = jnp.exp(A_cumsum)
            Y_off = jnp.einsum('bclhn,bchpn,bhcl->bclhp', Ch, states_prev, state_decay_out)
            Y = (Y_diag + Y_off).reshape(b, l, h, p) + x * Dskip[None, None, :, None]
            return Y

        def gated_rmsnorm(y, z, w):
            x = y * jax.nn.silu(z)
            gs = D_INNER // NGROUPS
            xg = x.reshape(x.shape[:-1] + (NGROUPS, gs))
            var = jnp.mean(xg * xg, axis=-1, keepdims=True)
            xg = xg * jax.lax.rsqrt(var + EPS)
            return xg.reshape(x.shape) * w[None, None, :]
        key = jax.random.key(seed)
        ks = jax.random.split(key, 9)
        B, L = (2, 512)
        return {'hidden_states': jax.random.normal(ks[0], (B, L, D_MODEL), jnp.float32), 'W_in': jax.random.normal(ks[1], (D_MODEL, D_IN_PROJ), jnp.float32) * 0.02, 'conv_w': jax.random.normal(ks[2], (CONV_DIM, D_CONV), jnp.float32) * 0.2, 'conv_b': jax.random.normal(ks[3], (CONV_DIM,), jnp.float32) * 0.02, 'A': -jnp.exp(jax.random.normal(ks[4], (NHEADS,), jnp.float32) * 0.5), 'D': jax.random.normal(ks[5], (NHEADS,), jnp.float32) * 0.5, 'dt_bias': jax.random.normal(ks[6], (NHEADS,), jnp.float32) * 0.5, 'norm_w': jnp.ones((D_INNER,), jnp.float32) + jax.random.normal(ks[7], (D_INNER,), jnp.float32) * 0.02, 'W_out': jax.random.normal(ks[8], (D_INNER, D_MODEL), jnp.float32) * 0.02}
    _L0_attn_in = _L0_attn_setup()

    def _L0_ffn_setup():
        import jax, jax.numpy as jnp
        import numpy as np
        H = 512
        I = 352
        E = 8
        TOP_K = 2
        N_SHARED = 2
        IS = N_SHARED * I
        key = jax.random.key(seed)
        ks = jax.random.split(key, 8)
        s_h = 1.0 / np.sqrt(H)
        s_i = 1.0 / np.sqrt(I)
        s_is = 1.0 / np.sqrt(IS)
        return {'hidden_states': jax.random.normal(ks[0], (1, 512, H), jnp.float32), 'gate_w': jax.random.normal(ks[1], (E, H), jnp.float32) * s_h, 'w_gate': jax.random.normal(ks[2], (E, H, I), jnp.float32) * s_h, 'w_up': jax.random.normal(ks[3], (E, H, I), jnp.float32) * s_h, 'w_down': jax.random.normal(ks[4], (E, I, H), jnp.float32) * s_i, 'sw_gate': jax.random.normal(ks[5], (H, IS), jnp.float32) * s_h, 'sw_up': jax.random.normal(ks[6], (H, IS), jnp.float32) * s_h, 'sw_down': jax.random.normal(ks[7], (IS, H), jnp.float32) * s_is}
    _L0_ffn_in = _L0_ffn_setup()
    _d = {'L0_attn_hidden_states': _L0_attn_in['hidden_states'], 'L0_attn_W_in': _L0_attn_in['W_in'], 'L0_attn_conv_w': _L0_attn_in['conv_w'], 'L0_attn_conv_b': _L0_attn_in['conv_b'], 'L0_attn_A': _L0_attn_in['A'], 'L0_attn_D': _L0_attn_in['D'], 'L0_attn_dt_bias': _L0_attn_in['dt_bias'], 'L0_attn_norm_w': _L0_attn_in['norm_w'], 'L0_attn_W_out': _L0_attn_in['W_out'], 'L0_ffn_gate_w': _L0_ffn_in['gate_w'], 'L0_ffn_w_gate': _L0_ffn_in['w_gate'], 'L0_ffn_w_up': _L0_ffn_in['w_up'], 'L0_ffn_w_down': _L0_ffn_in['w_down'], 'L0_ffn_sw_gate': _L0_ffn_in['sw_gate'], 'L0_ffn_sw_up': _L0_ffn_in['sw_up'], 'L0_ffn_sw_down': _L0_ffn_in['sw_down']}
    _x0 = _d['L0_attn_hidden_states']
    _d['L0_attn_hidden_states'] = jax.random.normal(jax.random.fold_in(jax.random.key(seed), 1), (8, 512, 512), dtype=_x0.dtype)
    del _x0
    return _d

def reference(L0_attn_hidden_states, L0_attn_W_in, L0_attn_conv_w, L0_attn_conv_b, L0_attn_A, L0_attn_D, L0_attn_dt_bias, L0_attn_norm_w, L0_attn_W_out, L0_ffn_gate_w, L0_ffn_w_gate, L0_ffn_w_up, L0_ffn_w_down, L0_ffn_sw_gate, L0_ffn_sw_up, L0_ffn_sw_down):

    def _L0_attn_ref(hidden_states, W_in, conv_w, conv_b, A, D, dt_bias, norm_w, W_out):
        import jax, jax.numpy as jnp
        import numpy as np
        D_MODEL = 512
        EXPAND = 2
        D_INNER = D_MODEL * EXPAND
        HEAD_DIM = 64
        NHEADS = D_INNER // HEAD_DIM
        D_STATE = 128
        NGROUPS = 1
        D_CONV = 4
        CHUNK = 64
        CONV_DIM = D_INNER + 2 * NGROUPS * D_STATE
        D_IN_PROJ = 2 * D_INNER + 2 * NGROUPS * D_STATE + NHEADS
        EPS = 1e-05

        def segsum(x):
            T = x.shape[-1]
            xc = jnp.cumsum(x, axis=-1)
            diff = xc[..., :, None] - xc[..., None, :]
            mask = jnp.tril(jnp.ones((T, T), dtype=bool))
            return jnp.where(mask, diff, -jnp.inf)

        def causal_conv1d(x, w, b):
            K = w.shape[1]
            L = x.shape[1]
            xp = jnp.pad(x, ((0, 0), (K - 1, 0), (0, 0)))
            y = b[None, None, :]
            for k in range(K):
                y = y + xp[:, k:k + L, :] * w[None, None, :, k]
            return jax.nn.silu(y)

        def ssd_chunked(x, dt, A, B, C, Dskip):
            b, l, h, p = x.shape
            g, n = (B.shape[2], B.shape[3])
            c = l // CHUNK
            xc = x.reshape(b, c, CHUNK, h, p)
            dtc = dt.reshape(b, c, CHUNK, h)
            Bh = jnp.repeat(B.reshape(b, c, CHUNK, g, n), h // g, axis=3)
            Ch = jnp.repeat(C.reshape(b, c, CHUNK, g, n), h // g, axis=3)
            dA = dtc * A[None, None, None, :]
            dAc = jnp.moveaxis(dA, 3, 1)
            A_cumsum = jnp.cumsum(dAc, axis=-1)
            Lmat = jnp.exp(segsum(dAc))
            Y_diag = jnp.einsum('bclhn,bcshn,bhcls,bcsh,bcshp->bclhp', Ch, Bh, Lmat, dtc, xc)
            decay_states = jnp.exp(A_cumsum[..., -1:] - A_cumsum)
            states = jnp.einsum('bclhn,bhcl,bclh,bclhp->bchpn', Bh, decay_states, dtc, xc)
            states = jnp.concatenate([jnp.zeros_like(states[:, :1]), states], axis=1)
            chunk_sums = jnp.pad(A_cumsum[..., -1], ((0, 0), (0, 0), (1, 0)))
            decay_chunk = jnp.exp(segsum(chunk_sums))
            new_states = jnp.einsum('bhzc,bchpn->bzhpn', decay_chunk, states)
            states_prev = new_states[:, :-1]
            state_decay_out = jnp.exp(A_cumsum)
            Y_off = jnp.einsum('bclhn,bchpn,bhcl->bclhp', Ch, states_prev, state_decay_out)
            Y = (Y_diag + Y_off).reshape(b, l, h, p) + x * Dskip[None, None, :, None]
            return Y

        def gated_rmsnorm(y, z, w):
            x = y * jax.nn.silu(z)
            gs = D_INNER // NGROUPS
            xg = x.reshape(x.shape[:-1] + (NGROUPS, gs))
            var = jnp.mean(xg * xg, axis=-1, keepdims=True)
            xg = xg * jax.lax.rsqrt(var + EPS)
            return xg.reshape(x.shape) * w[None, None, :]
        b, l, _ = hidden_states.shape
        zxbcdt = hidden_states @ W_in
        z = zxbcdt[..., :D_INNER]
        xbc = zxbcdt[..., D_INNER:D_INNER + CONV_DIM]
        dt = zxbcdt[..., D_INNER + CONV_DIM:]
        xbc = causal_conv1d(xbc, conv_w, conv_b)
        x = xbc[..., :D_INNER].reshape(b, l, NHEADS, HEAD_DIM)
        Bs = xbc[..., D_INNER:D_INNER + NGROUPS * D_STATE].reshape(b, l, NGROUPS, D_STATE)
        Cs = xbc[..., D_INNER + NGROUPS * D_STATE:].reshape(b, l, NGROUPS, D_STATE)
        dt = jax.nn.softplus(dt + dt_bias[None, None, :])
        y = ssd_chunked(x, dt, A, Bs, Cs, D).reshape(b, l, D_INNER)
        y = gated_rmsnorm(y, z, norm_w)
        return y @ W_out

    def _L0_ffn_ref(hidden_states, gate_w, w_gate, w_up, w_down, sw_gate, sw_up, sw_down):
        import jax, jax.numpy as jnp
        import numpy as np
        H = 512
        I = 352
        E = 8
        TOP_K = 2
        N_SHARED = 2
        IS = N_SHARED * I
        B, S, _ = hidden_states.shape
        x = hidden_states.reshape(-1, H)
        N = x.shape[0]
        logits = x @ gate_w.T
        scores = jax.nn.softmax(logits, axis=-1)
        topk_w, topk_i = jax.lax.top_k(scores, TOP_K)
        g = jnp.einsum('nh,ehi->eni', x, w_gate)
        u = jnp.einsum('nh,ehi->eni', x, w_up)
        h = jax.nn.silu(g) * u
        eo = jnp.einsum('eni,eih->enh', h, w_down)
        combine = jnp.zeros((N, E), x.dtype).at[jnp.arange(N)[:, None], topk_i].add(topk_w)
        y = jnp.einsum('ne,enh->nh', combine, eo)
        sh = jax.nn.silu(x @ sw_gate) * (x @ sw_up)
        y = y + sh @ sw_down
        return y.reshape(B, S, H)
    x = L0_attn_hidden_states
    xn = _layernorm(x, axis=-1)
    s = _L0_attn_ref(xn, L0_attn_W_in, L0_attn_conv_w, L0_attn_conv_b, L0_attn_A, L0_attn_D, L0_attn_dt_bias, L0_attn_norm_w, L0_attn_W_out)
    g = _silu(_L0_ffn_ref(xn, L0_ffn_gate_w, L0_ffn_w_gate, L0_ffn_w_up, L0_ffn_w_down, L0_ffn_sw_gate, L0_ffn_sw_up, L0_ffn_sw_down))
    x = x + s * g
    return x

_drawn_inputs = setup_inputs


def setup_inputs(seed=0):
    import zlib

    import numpy as np

    out = dict(_drawn_inputs(seed))
    spreads = {}
    factors = {'L0_attn_A': 7.005, 'L0_attn_dt_bias': 6.46, 'L0_attn_norm_w': 8.0}
    for name, (base, spread) in spreads.items():
        noise = np.random.default_rng([zlib.crc32(name.encode()), seed]).standard_normal(out[name].shape)
        drawn = base * np.exp(spread * noise) if base else spread * noise
        out[name] = jnp.asarray(drawn.astype(out[name].dtype))
    for name, factor in factors.items():
        out[name] = (out[name] * factor).astype(out[name].dtype)
    return out
```

```python
from contextlib import ExitStack

import concourse.bass as bass
from concourse import mybir

F32 = mybir.dt.float32
F32R = mybir.dt.float32r
U32 = mybir.dt.uint32
I32 = mybir.dt.int32
ALU = mybir.AluOpType
ACT = mybir.ActivationFunctionType
AX = mybir.AxisListType

P = 128
PARTS = ((0, 0), (0, 1), (1, 0))


class Ring:

    def __init__(self, uses, slots):
        self.at = {}
        self.per_slot = [0] * slots
        for n, name in enumerate(uses):
            self.at[name] = (n % slots, self.per_slot[n % slots])
            self.per_slot[n % slots] += 1


def program(nc, x, W_in, conv_w, conv_b, A, D, dt_bias, norm_w, W_out, gate_w, w_gate, w_up, w_down,
            sw_gate, sw_up, sw_down, out):
    B, L, H = x.shape
    N = B * L
    KH = H // P
    CONV, TAPS = conv_w.shape
    NHEADS = A.shape[0]
    INNER = norm_w.shape[0]
    HD = INNER // NHEADS
    STATE = (CONV - INNER) // 2
    E, _, I = w_gate.shape
    IS = sw_gate.shape[1]
    ZT, CT = INNER // P, CONV // P
    XT = INNER // P
    C = L // P
    NT = N // P
    HH = NHEADS // 2
    assert STATE == P and L == 512 and H == 512 and NHEADS + E <= P

    TOP = 2
    HALVES = 2
    PAIR = HALVES * P
    MIN_PAIRS = TOP * N // PAIR
    MAX_PAIRS = MIN_PAIRS + E - 1
    FETCH_AHEAD = 2
    NQ = HALVES * (MAX_PAIRS + FETCH_AHEAD)
    assert NQ <= P and TOP == 2

    y_dram = nc.dram_tensor("mixer_y", (B, C, P, XT * P), F32).ap()
    xn_dram = nc.dram_tensor("xn_rows", (N, H), F32).ap()

    eo_dram = nc.dram_tensor("expert_rows", (MAX_PAIRS * PAIR, H), F32).ap()
    eo_rows = eo_dram.rearrange("(t p) h -> t p h", p=P)

    x_tok = x.rearrange("b (c p) h -> b p c h", p=P)
    xn_tok = xn_dram.rearrange("(b c p) h -> b p c h", b=B, p=P)
    out_tok = out.rearrange("b (c p) h -> b p c h", p=P)

    outer = ExitStack()
    with outer:
        def keep(name, shape, dt=F32):
            return outer.enter_context(nc.sbuf_tensor(name, shape, dt))

        ident = keep("ident", [P, P])
        upto = keep("upto", [P, P])
        after = keep("after", [P, P])
        ones = keep("ones", [P, P])
        logits = keep("logits", [P, NT, E])
        const_made = outer.enter_context(nc.semaphore("const_made"))

        stage = ExitStack()
        with stage:
            def sb(name, shape, dt=F32):
                return stage.enter_context(nc.sbuf_tensor(name, shape, dt))

            def sem(name):
                return stage.enter_context(nc.semaphore(name))

            w_part = [sb(f"w_in_{p}", [P, KH, INNER + CONV], F32R) for p in ("hi", "lo")]
            dtg_part = [sb(f"w_dtg_{p}", [P, KH, P], F32R) for p in ("hi", "lo")]
            dtg_raw = sb("dtg_raw", [P, KH, P])
            after_r = sb("after_r", [P, P], F32R)
            cw = sb("cw", [P, CT, TAPS])
            cb = sb("cb", [P, CT])
            d_col = sb("d_col", [P, XT])
            a_row = sb("a_row", [P, NHEADS])
            bias_row = sb("bias_row", [P, NHEADS])
            xrow = sb("xrow", [P, C, H])
            xnT = [sb(f"xnT_{p}", [P, KH, L], F32R) for p in ("hi", "lo")]
            stats = sb("stats", [P, C, 6])
            mv = sb("mv", [P, C, 2])
            rstd = sb("rstd", [P, C])
            nwt = sb("nwt", [P, 3, C])
            acc = sb("acc", [P, 2, 2, L])
            xbc = sb("xbc", [P, CT, L])
            zs = sb("zs", [P, ZT, L])
            dtgT = sb("dtgT", [P, L])
            dt_, dA, dA_lo, dt_in, u, w1, ln_w, tmp = [
                sb(n, [P, C, NHEADS]) for n in ("dt", "dA", "dA_lo", "dt_in", "u", "w1", "ln_w", "dt_tmp")]
            dA_hi = sb("dA_hi", [P, C, NHEADS], F32R)
            nothing = sb("nothing", [P, 8])
            ex = sb("ex", [P, 3, C, NHEADS])
            seg_rhs = [sb(f"seg_rhs_{p}", [P, 2, HH, P], F32R) for p in ("hi", "lo")]
            decay = sb("decay", [P, 2, HH, P])
            cbm = sb("cbm", [P, P])
            btok = sb("btok", [P, P])
            xdt = sb("xdt", [P, INNER])
            xdec = sb("xdec", [P, INNER])
            state = sb("state", [P, INNER])
            yoff = sb("yoff", [P, INNER])
            ybuf = sb("ybuf", [P, 2, XT, P])

            psS = stage.enter_context(nc.psum_tensor("psS", [P, 2, 512], F32))
            psD = stage.enter_context(nc.psum_tensor("psD", [P, 3, 1024], F32))
            full = {k: [sem(f"ps{k}{i}_full") for i in range(n)] for k, n in (("S", 2), ("D", 3))}
            taken = {k: [sem(f"ps{k}{i}_taken") for i in range(n)] for k, n in (("S", 2), ("D", 3))}

            uses = {"S": ["dtg", "dtt", "sums"], "D": []}
            PAIRS = (ZT + CT) // 2
            FRONT_AT = PAIRS - 2

            def front(c):
                uses["S"].append(f"cb{c}")
                uses["D"].extend([f"xt{c}", f"seg{c}0", f"seg{c}1"])

            for j in range(PAIRS):
                if j == FRONT_AT:
                    front(0)
                uses["D"].append(f"p{j}")
            for c in range(C):
                if c:
                    uses["D"].append(f"off{c}")
                if c + 1 < C:
                    uses["D"].append(f"new{c}")
                uses["D"].append(f"y{c}")
                if c + 1 < C:
                    front(c + 1)
                uses["S"].append(f"xn{c}")
            rings = {"S": Ring(uses["S"], 2), "D": Ring(uses["D"], 3)}
            where = {n: (k, *v) for k, r in rings.items() for n, v in r.at.items()}
            if sum(len(r.at) for r in rings.values()) != len(where):
                raise ValueError("a PSUM use is named twice")

            param_loaded = sem("param_loaded")
            w_loaded = [sem("w0_loaded"), sem("w1_loaded")]
            zeros_made = sem("zeros_made")
            rows_zeroed = sem("rows_zeroed")
            w_hi = sem("w_hi")
            w_lo = sem("w_lo")
            x_loaded = sem("x_loaded")
            xn_stored = sem("xn_stored")
            ln_done = sem("ln_done")
            xn0_full = sem("xn0_full")
            xnT_hi = sem("xnT_hi")
            xnT_lo = sem("xnT_lo")
            tap3 = sem("tap3")
            xbc_done = sem("xbc_done")
            dt_neg = sem("dt_neg")
            dt_exp = sem("dt_exp")
            dt_one = sem("dt_one")
            dt_ln = sem("dt_ln")
            dA_done = sem("dA_done")
            seg_hi = sem("seg_hi")
            seg_lo = sem("seg_lo")
            cbm_done = sem("cbm_done")
            m_done = sem("m_done")
            xdec_done = sem("xdec_done")
            state_scaled = sem("state_scaled")
            y_done = sem("y_done")
            y_stored = [sem("y0_stored"), sem("y1_stored")]
            own = sem("own")

            XP = CT // 2
            OWN = 33
            NPARAM = 4 + NHEADS + 1 + KH
            WC = 576
            NW = (INNER + CONV) // WC
            w_raw = [xbc[:, 5 * i:5 * i + 5, :].rearrange("p t l -> p (t l)")[:, 0:KH * WC]
                     .rearrange("p (k n) -> p k n", k=KH) for i in range(2)]
            w_cols = W_in.rearrange("(k p) n -> p k n", p=P)
            W_ORDER = [*range(INNER // WC, NW), *range(INNER // WC)]

            def w_slice(n):
                return slice(W_ORDER[n] * WC, (W_ORDER[n] + 1) * WC)

            def w_needed(end):
                return 3 + max(W_ORDER.index((end - 1) // WC), W_ORDER.index((end - 2 * P) // WC))

            def ps(name):
                k, slot, _ = where[name]
                return (psS if k == "S" else psD)[:, slot, :]

            def is_full(name):
                k, slot, _ = where[name]
                return full[k][slot]

            def is_taken(name):
                k, slot, _ = where[name]
                return taken[k][slot]

            def wait_full(e, b, name):
                k, slot, n = where[name]
                e.wait_ge(full[k][slot], b * rings[k].per_slot[slot] + n + 1)

            def wait_room(e, b, name):
                k, slot, n = where[name]
                e.wait_ge(taken[k][slot], b * rings[k].per_slot[slot] + n + 1)

            def wait_taken(e, b, name):
                k, slot, n = where[name]
                e.wait_ge(taken[k][slot], b * rings[k].per_slot[slot] + n + 2)

            def by_head(row, n=HD):
                return row.unsqueeze(2).to_broadcast([P, row.shape[1], n])

            def heads(flat):
                return flat.rearrange("p (h d) -> p h d", d=HD)

            block = stage.enter_context(nc.Block())

            @block.gpsimd
            def _(pool):
                g = nc.gpsimd
                g.memset(ident[:, :], 0.0).then_inc(const_made, 1)
                g.memset(ones[:, :], 1.0).then_inc(const_made, 1)
                g.memset(dtg_raw[:, :, :], 0.0).then_inc(const_made, 1)
                g.memset(zs[:, :, :], 0.0).then_inc(zeros_made, 1)
                pool.wait_ge(const_made, 3)
                g.affine_select(out=ident[:, :], in_=ident[:, :], compare_op=ALU.not_equal, fill=1.0,
                                base=0, pattern=[[-1, P]], channel_multiplier=1).then_inc(const_made, 1)
                g.affine_select(out=upto[:, :], in_=ones[:, :], compare_op=ALU.is_ge, fill=0.0,
                                base=0, pattern=[[1, P]], channel_multiplier=-1).then_inc(const_made, 1)
                g.affine_select(out=after[:, :], in_=ones[:, :], compare_op=ALU.is_gt, fill=0.0,
                                base=0, pattern=[[-1, P]], channel_multiplier=1).then_inc(const_made, 1)
                pool.wait_ge(const_made, 6)
                pool.wait_ge(param_loaded, 16 * NPARAM)

                with pool.Fori(0, B) as b:
                    pool.wait_ge(dA_done, b + 1)

                    def masked(c):
                        for half in range(2):
                            if c:
                                wait_full(pool, b, f"seg{c - 1}{half}")
                            hs = slice(half * HH, (half + 1) * HH)
                            g.tensor_tensor(seg_rhs[0][:, half], upto[:, :].unsqueeze(1).to_broadcast([P, HH, P]),
                                            by_head(dA_hi[:, c, hs].bitcast(F32), P), ALU.mult).then_inc(seg_hi, 1)

                    masked(0)
                    for c in range(C - 1):
                        if c == 0:
                            wait_taken(pool, b, "sums")
                        else:
                            wait_full(pool, b, f"new{c - 1}")
                        wait_taken(pool, b, f"xt{c}")
                        g.tensor_tensor(heads(xdec[:, :]), heads(xdt[:, :]), by_head(ex[:, 1, c]),
                                        ALU.mult).then_inc(xdec_done, 1)
                        if c:
                            wait_full(pool, b, f"off{c}")
                            g.tensor_tensor(heads(state[:, :]), heads(state[:, :]), by_head(ex[:, 2, c]),
                                            ALU.mult).then_inc(state_scaled, 1)
                        masked(c + 1)

            @block.sync
            def _(sp):
                with nc.allow_non_contiguous_dma(reason="small parameter tables"):
                    sp.dma_start(xrow[:, :, :], x_tok[0]).then_inc(x_loaded, 16)
                    sp.dma_start(cw[:, :, :], conv_w.rearrange("(t p) k -> p t k", p=P)).then_inc(param_loaded, 16)
                    sp.dma_start(cb[:, :], conv_b.rearrange("(t p) -> p t", p=P)).then_inc(param_loaded, 16)
                    sp.dma_start(a_row[:, :], A.partition_broadcast(P)).then_inc(param_loaded, 16)
                    sp.dma_start(bias_row[:, :], dt_bias.partition_broadcast(P)).then_inc(param_loaded, 16)
                    for n in range(2):
                        sp.dma_start(w_raw[n], w_cols[:, :, w_slice(n)]).then_inc(w_loaded[n], 16)
                    for h in range(NHEADS):
                        j, i = h // (P // HD), h % (P // HD)
                        sp.dma_start(d_col[i * HD:(i + 1) * HD, j:j + 1],
                                     D[h:h + 1].partition_broadcast(HD)).then_inc(param_loaded, 16)
                    sp.wait_ge(const_made, 3)
                    sp.dma_start(dtg_raw[:, :, 0:NHEADS], w_cols[:, :, INNER + CONV:]).then_inc(param_loaded, 16)
                    for k in range(KH):
                        sp.dma_start(dtg_raw[:, k, NHEADS:NHEADS + E],
                                     gate_w[:, k * P:(k + 1) * P].rearrange("e p -> p e")).then_inc(param_loaded, 16)
                for n in range(2, NW):
                    sp.wait_ge(w_lo, n + 1)
                    sp.dma_start(w_raw[n % 2], w_cols[:, :, w_slice(n)]).then_inc(w_loaded[n % 2], 16)

                sp.wait_ge(zeros_made, 1)
                spare = eo_dram[MIN_PAIRS * PAIR:, :].rearrange("(a p r) n -> a p (r n)", a=2, p=P)
                for n in range(2):
                    sp.dma_start(spare[n], zs[:, :, :].rearrange("p t l -> p (t l)")[:, 0:spare.shape[2]]
                                 ).then_inc(rows_zeroed, 16)

                with sp.Fori(0, B) as b:
                    sp.wait_ge(ln_done, b + 1)
                    sp.dma_start(xn_tok[b], xrow[:, :, :]).then_inc(xn_stored, 16)
                    sp.wait_ge(xn_stored, b * 16 + 16)
                    sp.wait_ge(xnT_lo, b * KH + KH)
                    sp.dma_start(xrow[:, :, :], x_tok[(b + 1) % B]).then_inc(x_loaded, 16)
                    for c in range(C):
                        sp.wait_ge(y_done, b * C + c + 1)
                        sp.dma_start(y_dram[b, c], ybuf[:, c % 2].rearrange("p j l -> p (j l)")
                                     ).then_inc(y_stored[c % 2], 16)
                for i in range(2):
                    sp.wait_ge(y_stored[i], 16 + 16 * B * C // 2)

            @block.tensor
            def _(pe):
                t = nc.tensor

                def project(dst, w, j):
                    n = 0
                    for k in range(KH):
                        for s, m in PARTS:
                            ins = t.matmul(dst, w[s][:, k, j * P:(j + 1) * P], xnT[m][:, k, :],
                                           start=(n == 0), stop=(n == 3 * KH - 1))
                            n += 1
                    return ins

                def turn_x(dst, k):
                    for c in range(C):
                        ins = t.transpose(dst[:, c * P:(c + 1) * P], xrow[:, c, k * P:(k + 1) * P], ident[:, :])
                    return ins

                pe.wait_ge(const_made, 6)
                pe.wait_ge(ln_done, 1)
                for k in range(KH):
                    if k >= 2:
                        pe.wait_ge(xnT_lo, k - 1)
                    turn_x(psS[:, k % 2, :], k).then_inc(xn0_full, 1)
                pe.wait_ge(w_lo, 2)

                with pe.Fori(0, B) as b:
                    def front(c):
                        cols = slice(c * P, (c + 1) * P)
                        if c == 0:
                            pe.wait_ge(xbc_done, b * XP + XP)
                        wait_room(pe, b, f"cb{c}")
                        t.matmul(ps(f"cb{c}")[:, 0:P], xbc[:, XT, cols], xbc[:, XT + 1, cols],
                                 start=True, stop=True)
                        t.transpose(ps(f"cb{c}")[:, P:2 * P], xbc[:, XT, cols], ident[:, :]
                                    ).then_inc(is_full(f"cb{c}"), 1)
                        wait_room(pe, b, f"xt{c}")
                        for j in range(XT):
                            ins = t.transpose(ps(f"xt{c}")[:, j * P:(j + 1) * P], xbc[:, j, cols], ident[:, :])
                        ins.then_inc(is_full(f"xt{c}"), 1)
                        for half in range(2):
                            name = f"seg{c}{half}"
                            wait_room(pe, b, name)
                            pe.wait_ge(seg_hi, b * 2 * C + 2 * c + half + 1)
                            pe.wait_ge(seg_lo, b * 2 * C + 2 * c + half + 1)
                            for q in range(2):
                                hs = slice(q * HH // 2, (q + 1) * HH // 2)
                                for part in range(2):
                                    ins = t.matmul(ps(name)[:, q * 512:(q + 1) * 512], after_r[:, :],
                                                   seg_rhs[part][:, half, hs, :].rearrange("p h l -> p (h l)"),
                                                   start=(part == 0), stop=(part == 1))
                            ins.then_inc(is_full(name), 1)

                    def turn_next(c):
                        if c == 0:
                            pe.wait_ge(ln_done, b + 2)
                        wait_room(pe, b, f"xn{c}")
                        turn_x(ps(f"xn{c}"), c).then_inc(is_full(f"xn{c}"), 1)

                    pe.wait_ge(xnT_lo, b * KH + KH)
                    wait_room(pe, b, "dtg")
                    project(ps("dtg"), dtg_part, 0).then_inc(is_full("dtg"), 1)
                    for j in range(PAIRS):
                        if j == FRONT_AT:
                            front(0)
                        first = ZT + 2 * j if j < XP else 2 * (j - XP)
                        wait_room(pe, b, f"p{j}")
                        pe.wait_ge(w_lo, w_needed((first + 2) * P))
                        for i in range(2):
                            ins = project(ps(f"p{j}")[:, i * L:(i + 1) * L], w_part, first + i)
                        ins.then_inc(is_full(f"p{j}"), 1)
                        if j == 0:
                            wait_taken(pe, b, "dtg")
                            wait_room(pe, b, "dtt")
                            for c in range(C):
                                ins = t.transpose(ps("dtt")[:, c * P:(c + 1) * P], dtgT[:, c * P:(c + 1) * P],
                                                  ident[:, :])
                            ins.then_inc(is_full("dtt"), 1)
                        if j == XP:
                            pe.wait_ge(dA_done, b + 1)
                            wait_room(pe, b, "sums")
                            for i, m in enumerate((upto, after, ones)):
                                ins = t.matmul(ps("sums")[:, i * C * NHEADS:(i + 1) * C * NHEADS], m[:, :],
                                               dA[:, :, :].rearrange("p c h -> p (c h)"), start=True, stop=True)
                            ins.then_inc(is_full("sums"), 1)

                    for c in range(C):
                        cols = slice(c * P, (c + 1) * P)
                        if c:
                            wait_taken(pe, b, f"new{c - 1}")
                            wait_room(pe, b, f"off{c}")
                            for q in range(2):
                                ins = t.matmul(ps(f"off{c}")[:, q * 512:(q + 1) * 512], xbc[:, XT + 1, cols],
                                               state[:, q * 512:(q + 1) * 512], start=True, stop=True)
                            ins.then_inc(is_full(f"off{c}"), 1)
                        if c + 1 < C:
                            wait_taken(pe, b, f"cb{c}")
                            pe.wait_ge(xdec_done, b * (C - 1) + c + 1)
                            wait_room(pe, b, f"new{c}")
                            for q in range(2):
                                ins = t.matmul(ps(f"new{c}")[:, q * 512:(q + 1) * 512], btok[:, :],
                                               xdec[:, q * 512:(q + 1) * 512], start=True, stop=True)
                            ins.then_inc(is_full(f"new{c}"), 1)
                        else:
                            turn_next(c)
                        wait_room(pe, b, f"y{c}")
                        wait_taken(pe, b, f"xt{c}")
                        for half in range(2):
                            pe.wait_ge(m_done, b * 2 * C + 2 * c + half + 1)
                            for j in range(half * XT // 2, (half + 1) * XT // 2):
                                for i in range(P // HD):
                                    h = j * (P // HD) + i
                                    ins = t.matmul(ps(f"y{c}")[i * HD:(i + 1) * HD, j * P:(j + 1) * P],
                                                   xdt[:, h * HD:(h + 1) * HD], decay[:, half, h % HH, :],
                                                   start=True, stop=(c == 0), skip_group_check=True)
                                if c:
                                    if j == 0:
                                        wait_taken(pe, b, f"off{c}")
                                    ins = t.matmul(ps(f"y{c}")[:, j * P:(j + 1) * P],
                                                   yoff[:, j * P:(j + 1) * P], ident[:, :],
                                                   start=False, stop=True, skip_group_check=True)
                        ins.then_inc(is_full(f"y{c}"), 1)
                        if c + 1 < C:
                            front(c + 1)
                        if c + 1 < C:
                            turn_next(c)

            @block.scalar
            def _(act):
                s = nc.scalar
                act.wait_ge(param_loaded, 16 * NPARAM)
                s.activation(dtg_part[0][:, :, :], dtg_raw[:, :, :], ACT.Copy).then_inc(w_hi, 1)
                for k in range(KH):
                    act.wait_ge(xn0_full, k + 1)
                    s.activation(xnT[0][:, k, :], psS[:, k % 2, :], ACT.Copy).then_inc(xnT_hi, 1)
                for n in range(NW):
                    act.wait_ge(w_loaded[n % 2], 16 * (n // 2 + 1))
                    s.activation(w_part[0][:, :, w_slice(n)], w_raw[n % 2], ACT.Copy).then_inc(w_hi, 1)

                act.wait_ge(rows_zeroed, 32)
                with act.Fori(0, B) as b:
                    def tap(j):
                        wait_full(act, b, f"p{j}")
                        if j >= 2:
                            act.wait_ge(xbc_done, b * XP + j - 1)
                        for i in range(2):
                            ct = 2 * j + i
                            ins = s.activation(acc[:, j % 2, i, :], ps(f"p{j}")[:, i * L:(i + 1) * L],
                                               ACT.Identity, bias=cb[:, ct:ct + 1], scale=cw[:, ct, TAPS - 1:TAPS])
                        ins.then_inc(tap3, 1)

                    def masked(c, half):
                        for i in range(HH):
                            h = half * HH + i
                            ins = s.activation(seg_rhs[1][:, half, i, :], upto[:, :], ACT.Copy,
                                               scale=dA_lo[:, c, h:h + 1])
                        ins.then_inc(seg_lo, 1)

                    def exponents():
                        wait_full(act, b, "sums")
                        s.activation(ex[:, :, :, :].rearrange("p a c h -> p (a c h)"),
                                     ps("sums")[:, 0:3 * C * NHEADS], ACT.Exp).then_inc(is_taken("sums"), 1)

                    def front(c):
                        wait_full(act, b, f"cb{c}")
                        act.wait_ge(cbm_done, b * C + c + 1)
                        if c:
                            wait_full(act, b, f"new{c - 1}")
                        s.activation(btok[:, :], ps(f"cb{c}")[:, P:2 * P], ACT.Copy).then_inc(is_taken(f"cb{c}"), 1)
                        for half in range(2):
                            if c and not half:
                                wait_full(act, b, f"y{c - 1}")
                            wait_full(act, b, f"seg{c}{half}")
                            s.activation(decay[:, half].rearrange("p h l -> p (h l)"), ps(f"seg{c}{half}"),
                                         ACT.Exp).then_inc(is_taken(f"seg{c}{half}"), 1)

                    wait_full(act, b, "dtg")
                    s.activation(dtgT[:, :], ps("dtg"), ACT.Copy).then_inc(is_taken("dtg"), 1)
                    tap(0)
                    act.wait_ge(dt_neg, b + 1)
                    s.activation(u[:, :, :], tmp[:, :, :], ACT.Exp).then_inc(dt_exp, 1)
                    tap(1)
                    act.wait_ge(dt_one, b + 1)
                    s.activation(ln_w[:, :, :], w1[:, :, :], ACT.Ln).then_inc(dt_ln, 1)
                    for j in range(XP):
                        wait_taken(act, b, f"p{j}")
                        s.activation(xbc[:, 2 * j:2 * j + 2, :], acc[:, j % 2, :, :], ACT.Silu
                                     ).then_inc(xbc_done, 1)
                        if j + 2 < XP:
                            tap(j + 2)
                    act.wait_ge(dA_done, b + 1)
                    for half in range(2):
                        masked(0, half)
                    for j in range(XP, PAIRS):
                        if j == XP + 1:
                            exponents()
                        if j == FRONT_AT:
                            front(0)
                            for half in range(2):
                                masked(1, half)
                        wait_full(act, b, f"p{j}")
                        i = 2 * (j - XP)
                        s.activation(zs[:, i:i + 2, :].rearrange("p t l -> p (t l)"), ps(f"p{j}"), ACT.Silu
                                     ).then_inc(is_taken(f"p{j}"), 1)
                    for c in range(C):
                        if c + 1 < C:
                            front(c + 1)
                        wait_full(act, b, f"xn{c}")
                        s.activation(xnT[0][:, c, :], ps(f"xn{c}"), ACT.Copy).then_inc(xnT_hi, 1)
                        if c + 2 < C:
                            for half in range(2):
                                masked(c + 2, half)

            @block.vector
            def _(dve):
                v = nc.vector
                for n, slot in enumerate(taken["S"] + taken["D"]):
                    v.memset(nothing[:, n:n + 1], 0.0).then_inc(slot, 1)
                for i in range(2):
                    v.memset(nothing[:, 5 + i:6 + i], 0.0).then_inc(y_stored[i], 16)

                n_own = [0, 0]

                def then_read(ins):
                    n_own[0] += 1
                    ins.then_inc(own, 1)
                    dve.wait_ge(own, n_own[1] + n_own[0])

                def layernorm(n):
                    dve.wait_ge(x_loaded, n * 16)
                    for c in range(C):
                        ins = v.bn_stats(stats[:, c, :], xrow[:, c, :])
                    then_read(ins)
                    v.memset(nothing[:, 7:8], 0.0)
                    for c in range(C):
                        ins = v.bn_aggr(mv[:, c, :], stats[:, c, :])
                    then_read(ins)
                    then_read(v.tensor_scalar(nwt[:, 0, :], mv[:, :, 1], 1e-5, None, ALU.add))
                    then_read(v.tensor_scalar(rstd[:, :].bitcast(I32), nwt[:, 0, :].bitcast(I32),
                                              -0.5, 1597463007.0, ALU.mult, ALU.add))
                    for _ in range(4):
                        then_read(v.tensor_tensor(nwt[:, 1, :], rstd[:, :], rstd[:, :], ALU.mult))
                        then_read(v.scalar_tensor_tensor(out=nwt[:, 2, :], in0=nwt[:, 1, :], scalar=-0.5,
                                                         in1=nwt[:, 0, :], op0=ALU.mult, op1=ALU.mult))
                        then_read(v.scalar_tensor_tensor(out=rstd[:, :], in0=nwt[:, 2, :], scalar=1.5,
                                                         in1=rstd[:, :], op0=ALU.add, op1=ALU.mult))
                    for c in range(C):
                        ins = v.tensor_scalar(xrow[:, c, :], xrow[:, c, :], mv[:, c, 0:1], rstd[:, c:c + 1],
                                              ALU.subtract, ALU.mult)
                    ins.then_inc(ln_done, 1)

                layernorm(1)
                for k in range(KH):
                    dve.wait_ge(xnT_hi, k + 1)
                    v.tensor_tensor(xnT[1][:, k, :], psS[:, k % 2, :], xnT[0][:, k, :].bitcast(F32),
                                    ALU.subtract).then_inc(xnT_lo, 1)
                dve.wait_ge(w_hi, 1)
                v.tensor_tensor(dtg_part[1][:, :, :], dtg_raw[:, :, :], dtg_part[0][:, :, :].bitcast(F32),
                                ALU.subtract).then_inc(w_lo, 1)
                dve.wait_ge(const_made, 6)
                v.tensor_copy(after_r[:, :], after[:, :]).then_inc(w_lo, 1)
                for n in range(NW):
                    dve.wait_ge(w_hi, n + 2)
                    cols = w_slice(n)
                    v.tensor_tensor(w_part[1][:, :, cols], w_raw[n % 2], w_part[0][:, :, cols].bitcast(F32),
                                    ALU.subtract).then_inc(w_lo, 1)
                before_loop = n_own[0]

                with dve.Fori(0, B) as b:
                    n_own[:] = [before_loop, b * OWN]

                    def conv_pair(j):
                        dve.wait_ge(tap3, b * XP + j + 1)
                        for tap in range(TAPS - 2, -1, -1):
                            sh = TAPS - 1 - tap
                            for i in range(2):
                                ct = 2 * j + i
                                a = acc[:, j % 2, i, sh:L]
                                ins = v.scalar_tensor_tensor(out=a, in0=ps(f"p{j}")[:, i * L:(i + 1) * L - sh],
                                                             scalar=cw[:, ct, tap:tap + 1], in1=a,
                                                             op0=ALU.mult, op1=ALU.add)
                            if tap:
                                then_read(ins)
                        ins.then_inc(is_taken(f"p{j}"), 1)

                    def turned(c):
                        dve.wait_ge(xnT_hi, b * KH + KH + c + 1)
                        v.tensor_tensor(xnT[1][:, c, :], ps(f"xn{c}"), xnT[0][:, c, :].bitcast(F32),
                                        ALU.subtract).then_inc(xnT_lo, 1)
                        dve.wait_ge(xnT_lo, b * KH + KH + c + 1)
                        v.memset(nothing[:, 7:8], 0.0).then_inc(is_taken(f"xn{c}"), 1)

                    wait_full(dve, b, "dtt")
                    got = ps("dtt").rearrange("p (c n) -> p c n", n=P)
                    v.tensor_copy(logits[:, bass.ds(b * C, C), :], got[:, :, NHEADS:NHEADS + E])
                    v.tensor_tensor(dt_in[:, :, :], got[:, :, 0:NHEADS],
                                    bias_row[:, :].unsqueeze(1).to_broadcast([P, C, NHEADS]), ALU.add
                                    ).then_inc(is_taken("dtt"), 1)
                    wait_taken(dve, b, "dtt")
                    v.scalar_tensor_tensor(out=tmp[:, :, :], in0=dt_in[:, :, :], scalar=-1.0, in1=dt_in[:, :, :],
                                           op0=ALU.mult, op1=ALU.min).then_inc(dt_neg, 1)
                    conv_pair(0)
                    dve.wait_ge(dt_exp, b + 1)
                    v.tensor_scalar(w1[:, :, :], u[:, :, :], 1.0, None, ALU.add).then_inc(dt_one, 1)
                    conv_pair(1)
                    v.reciprocal(dA[:, :, :], w1[:, :, :])
                    then_read(v.tensor_scalar(tmp[:, :, :], w1[:, :, :], -1.0, None, ALU.add))
                    then_read(v.tensor_tensor(tmp[:, :, :], u[:, :, :], tmp[:, :, :], ALU.subtract))
                    then_read(v.tensor_tensor(tmp[:, :, :], tmp[:, :, :], dA[:, :, :], ALU.mult))
                    dve.wait_ge(dt_ln, b + 1)
                    then_read(v.tensor_tensor(tmp[:, :, :], tmp[:, :, :], ln_w[:, :, :], ALU.add))
                    then_read(v.scalar_tensor_tensor(out=dt_[:, :, :], in0=dt_in[:, :, :], scalar=0.0,
                                                     in1=tmp[:, :, :], op0=ALU.max, op1=ALU.add))
                    then_read(v.tensor_tensor(dA[:, :, :], dt_[:, :, :],
                                              a_row[:, :].unsqueeze(1).to_broadcast([P, C, NHEADS]), ALU.mult))
                    then_read(v.tensor_copy(dA_hi[:, :, :], dA[:, :, :]))
                    v.tensor_tensor(dA_lo[:, :, :], dA[:, :, :], dA_hi[:, :, :].bitcast(F32), ALU.subtract
                                    ).then_inc(dA_done, 1)
                    for j in range(2, XP):
                        conv_pair(j)

                    def state_part(c):
                        wait_full(dve, b, f"off{c}")
                        if c == 1:
                            wait_taken(dve, b, "sums")
                        v.tensor_tensor(heads(yoff[:, :]), heads(ps(f"off{c}")), by_head(ex[:, 0, c]), ALU.mult
                                        ).then_inc(is_taken(f"off{c}"), 1)

                    def gate_y(c):
                        wait_taken(dve, b, f"y{c}")
                        y = ybuf[:, c % 2]
                        v.tensor_tensor(y, y, zs[:, :, c * P:(c + 1) * P], ALU.mult).then_inc(y_done, 1)

                    def front(c):
                        wait_full(dve, b, f"cb{c}")
                        v.tensor_tensor(cbm[:, :], ps(f"cb{c}")[:, 0:P], upto[:, :], ALU.mult).then_inc(cbm_done, 1)
                        wait_full(dve, b, f"xt{c}")
                        if c:
                            wait_full(dve, b, f"y{c - 1}")
                            dve.wait_ge(xdec_done, b * (C - 1) + c)
                        v.tensor_tensor(heads(xdt[:, :]), heads(ps(f"xt{c}")), by_head(dt_[:, c]), ALU.mult
                                        ).then_inc(is_taken(f"xt{c}"), 1)
                        for half in range(2):
                            if half and c:
                                state_part(c)
                            wait_taken(dve, b, f"seg{c}{half}")
                            if not half:
                                dve.wait_ge(cbm_done, b * C + c + 1)
                            v.tensor_tensor(decay[:, half], decay[:, half],
                                            cbm[:, :].unsqueeze(1).to_broadcast([P, HH, P]), ALU.mult
                                            ).then_inc(m_done, 1)

                    front(0)
                    layernorm(b + 2)
                    for c in range(C):
                        if c + 1 < C:
                            if c:
                                dve.wait_ge(state_scaled, b * (C - 2) + c)
                            wait_full(dve, b, f"new{c}")
                            if c:
                                ins = v.tensor_tensor(state[:, :], ps(f"new{c}"), state[:, :], ALU.add)
                            else:
                                ins = v.tensor_copy(state[:, :], ps(f"new{c}"))
                            ins.then_inc(is_taken(f"new{c}"), 1)
                        if c:
                            gate_y(c - 1)
                            turned(c - 1)
                        if c + 1 == C:
                            turned(c)
                        wait_full(dve, b, f"y{c}")
                        dve.wait_ge(y_stored[c % 2], (b * (C // 2) + c // 2 + 1) * 16)
                        for j in range(XT):
                            ins = v.scalar_tensor_tensor(out=ybuf[:, c % 2, j, :], in0=xbc[:, j, c * P:(c + 1) * P],
                                                         scalar=d_col[:, j:j + 1],
                                                         in1=ps(f"y{c}")[:, j * P:(j + 1) * P],
                                                         op0=ALU.mult, op1=ALU.add)
                        ins.then_inc(is_taken(f"y{c}"), 1)
                        if c + 1 < C:
                            front(c + 1)
                    gate_y(C - 1)
                    assert n_own[0] - before_loop == OWN, n_own[0] - before_loop

        weight = [keep(f"weight_{k}", [P, NT]) for k in range(TOP)]
        row_of = [keep(f"row_of_{k}", [P, NT], U32) for k in range(TOP)]
        token_of = keep("token_of", [P, NQ], U32)
        first_pair = keep("first_pair", [P, E + 1], I32)

        KI = -(-I // P)
        GU = KH * 2 * I
        WS = GU + KI * H
        SL = IS // I
        FULL_COLS = GU + (I // P) * H
        REST = I - (I // P) * P
        DVE_COLS = FULL_COLS // 2 // 16 * 16
        WE_PIECES = ((slice(0, P), slice(0, FULL_COLS)), (slice(0, REST), slice(FULL_COLS, WS)))
        WE_SHARES = (((slice(0, P), slice(0, DVE_COLS)),), ((slice(0, P), slice(DVE_COLS, FULL_COLS)), WE_PIECES[1]))
        assert IS == SL * I and PAIR <= 256
        ws = [keep(f"ws_{p}", [P, SL, WS], F32R) for p in ("hi", "lo")]
        experts_weights = outer.enter_context(ExitStack())
        we = [[experts_weights.enter_context(nc.sbuf_tensor(f"we_{p}{i}", [P, WS], F32R)) for p in ("hi", "lo")]
              for i in range(2)]
        we_raw = experts_weights.enter_context(nc.sbuf_tensor("we_raw", [P, WS], F32))

        def k_rows(j):
            return min(P, I - j * P)

        def load_weights(e, dst, w_g, w_u, w_d, loaded):
            gu = dst[:, 0:GU].rearrange("p (k g i) -> p k g i", k=KH, g=2)
            e.dma_start(gu[:, :, 0, :], w_g.rearrange("(k p) i -> p k i", p=P)).then_inc(loaded, 16)
            e.dma_start(gu[:, :, 1, :], w_u.rearrange("(k p) i -> p k i", p=P)).then_inc(loaded, 16)
            full = I // P
            e.dma_start(dst[:, GU:FULL_COLS].rearrange("p (k n) -> p k n", k=full),
                        w_d[0:full * P, :].rearrange("(k p) n -> p k n", p=P)).then_inc(loaded, 16)
            e.dma_start(dst[0:REST, FULL_COLS:], w_d[full * P:I, :]).then_inc(loaded, 16)

        def load_expert(e, dst, n, loaded):
            load_weights(e, dst, w_gate[n], w_up[n], w_down[n], loaded)

        stage = ExitStack()
        with stage:
            def sb(name, shape, dt=F32):
                return stage.enter_context(nc.sbuf_tensor(name, shape, dt))

            def sem(name):
                return stage.enter_context(nc.semaphore(name))

            GROUP = 8
            NG = TOP * NT // GROUP
            iota_e = sb("iota_e", [P, E])
            iota_q = sb("iota_q", [P, P])
            token_id = sb("token_id", [P, NT])
            best = sb("best", [P, NT, 8])
            best_at = sb("best_at", [P, NT, 8], U32)
            choice = sb("choice", [P, TOP, NT])
            picked = [sb(f"picked_{k}", [P, E, NT]) for k in range(TOP)]
            either = sb("either", [P, E, NT])
            shifted = sb("shifted", [P, NT, E])
            total = sb("total", [P, NT])
            one_row = sb("one_row", [P, E * NT])
            tile_sum = sb("tile_sum", [P, E, NT])
            before = sb("before", [P, E, NT])
            upto_sum = sb("upto_sum", [P, E, NT])
            pairs = sb("pairs", [P, E])
            pair_end = sb("pair_end", [P, E + 1])
            base = sb("base", [P, E, NT])
            rows = sb("rows", [P, TOP, NT])
            tile_q = sb("tile_q", [P, TOP, NT])
            tile_r = sb("tile_r", [P, TOP, NT])
            hot_r = sb("hot_r", [P, 2, GROUP, P], F32R)
            hot_q = sb("hot_q", [P, 2, GROUP, NQ], F32R)
            psR = stage.enter_context(nc.psum_tensor("psR", [P, 3, 512], F32))

            iotas = sem("iotas")
            own = sem("r_own")
            picks = sem("picks")
            shifted_done = sem("shifted_done")
            var_done = sem("var_done")
            exp_done = sem("r_exp")
            counted = sem("counted")
            hot = sem("hot")
            placed = sem("placed")
            w_in = [sem(f"r_w{n}_loaded") for n in range(SL + 1)]
            w_hi = sem("r_w_hi")
            w_lo = sem("r_w_lo")
            w_sets = [(we[0][0][:, :], we[0][1][:, :])] + [(ws[0][:, n, :], ws[1][:, n, :]) for n in range(SL)]
            w_raw = [sb("r_w_raw", [P, WS]), we_raw]
            ROUND = 12582912.0
            block = stage.enter_context(nc.Block())

            @block.gpsimd
            def _(pool):
                g = nc.gpsimd
                g.iota(iota_e[:, :], pattern=[[1, E]], base=0, channel_multiplier=0,
                       allow_small_or_imprecise_dtypes=True).then_inc(iotas, 1)
                g.iota(iota_q[:, :], pattern=[[1, P]], base=0, channel_multiplier=0,
                       allow_small_or_imprecise_dtypes=True).then_inc(iotas, 1)
                g.iota(token_id[:, :], pattern=[[P, NT]], base=0, channel_multiplier=1,
                       allow_small_or_imprecise_dtypes=True).then_inc(iotas, 1)
                for n, (hi, lo) in enumerate(w_sets):
                    pool.wait_ge(w_hi, n + 1)
                    for rows, cols in WE_PIECES:
                        ins = g.tensor_tensor(lo[rows, cols], w_raw[n % 2][rows, cols],
                                              hi[rows, cols].bitcast(F32), ALU.subtract)
                    ins.then_inc(w_lo, 1)
                pool.wait_ge(w_lo, len(w_sets))

            @block.sync
            def _(sp):
                load_expert(sp, w_raw[0], 0, w_in[0])
                for n in range(SL):
                    cols = slice(n * I, (n + 1) * I)
                    if n:
                        sp.wait_ge(w_lo, n)
                    load_weights(sp, w_raw[(n + 1) % 2], sw_gate[:, cols], sw_up[:, cols], sw_down[cols, :],
                                 w_in[n + 1])

            @block.scalar
            def _(act):
                s = nc.scalar
                act.wait_ge(shifted_done, 1)
                s.activation(shifted[:, :, :], shifted[:, :, :], ACT.Exp).then_inc(exp_done, 1)
                for n, (hi, lo) in enumerate(w_sets):
                    act.wait_ge(w_in[n], 64)
                    for rows, cols in WE_PIECES:
                        ins = s.activation(hi[rows, cols], w_raw[n % 2][rows, cols], ACT.Copy)
                    ins.then_inc(w_hi, 1)

            @block.tensor
            def _(pe):
                t = nc.tensor
                pe.wait_ge(picks, 1)
                flat = either[:, :, :].rearrange("p e t -> p (e t)")
                t.matmul(psR[:, 0, 0:E * NT], upto[:, :], flat, start=True, stop=True)
                t.matmul(psR[:, 1, 0:E * NT], ones[:, :], flat, start=True, stop=True).then_inc(counted, 1)
                for n in range(NG):
                    pe.wait_ge(hot, n + 1)
                    for i in range(GROUP):
                        ins = t.matmul(psR[:, 2, 0:NQ], hot_r[:, n % 2, i, :], hot_q[:, n % 2, i, :],
                                       start=(n == 0 and i == 0), stop=(n == NG - 1 and i == GROUP - 1))
                    ins.then_inc(placed, 1)

            @block.vector
            def _(dve):
                v = nc.vector
                n_own = [0]

                def then_read(ins):
                    n_own[0] += 1
                    ins.then_inc(own, 1)
                    dve.wait_ge(own, n_own[0])

                for t in range(NT):
                    ins = v.max(best[:, t, :], logits[:, t, :])
                then_read(ins)
                v.tensor_tensor(shifted[:, :, :], logits[:, :, :], best[:, :, 0:1].to_broadcast([P, NT, E]),
                                ALU.subtract).then_inc(shifted_done, 1)
                for t in range(NT):
                    ins = v.max_index(best_at[:, t, :], best[:, t, :], logits[:, t, :])
                v.memset(one_row[:, :], 1.0)
                then_read(ins)
                then_read(v.tensor_copy(choice[:, :, :], best_at[:, :, 0:TOP].rearrange("p t k -> p k t")))
                dve.wait_ge(iotas, 3)
                for k in range(TOP):
                    ins = v.tensor_tensor(picked[k][:, :, :], iota_e[:, :].unsqueeze(2).to_broadcast([P, E, NT]),
                                          choice[:, k].unsqueeze(1).to_broadcast([P, E, NT]), ALU.is_equal)
                then_read(ins)
                v.tensor_tensor(either[:, :, :], picked[0][:, :, :], picked[1][:, :, :], ALU.add).then_inc(picks, 1)
                dve.wait_ge(exp_done, 1)
                then_read(v.tensor_reduce(total[:, :], shifted[:, :, :], AX.X, ALU.add))
                then_read(v.reciprocal(weight[0][:, :], total[:, :]))
                then_read(v.tensor_tensor(base[:, :, :], picked[1][:, :, :],
                                          shifted[:, :, :].rearrange("p t e -> p e t"), ALU.mult))
                then_read(v.tensor_reduce(weight[1][:, :], base[:, :, :].rearrange("p e t -> p t e"), AX.X, ALU.add))
                then_read(v.tensor_tensor(weight[1][:, :], weight[1][:, :], weight[0][:, :], ALU.mult))
                dve.wait_ge(counted, 1)
                flat = [x[:, :, :].rearrange("p e t -> p (e t)") for x in (tile_sum, upto_sum, before)]
                then_read(v.tensor_copy(flat[0], psR[:, 1, 0:E * NT]))
                then_read(v.tensor_tensor_scan(flat[1], one_row[:, :], flat[0], 0.0, ALU.mult, ALU.add))
                then_read(v.tensor_tensor(flat[2], flat[1], flat[0], ALU.subtract))
                then_read(v.tensor_tensor(pairs[:, :], upto_sum[:, :, NT - 1], before[:, :, 0], ALU.subtract))
                then_read(v.tensor_scalar(pairs[:, :], pairs[:, :], 1.0 / PAIR, 0.5 - 0.5 / PAIR, ALU.mult, ALU.add))
                then_read(v.tensor_scalar(pairs[:, :], pairs[:, :], ROUND, None, ALU.add))
                then_read(v.tensor_scalar(pairs[:, :], pairs[:, :], -ROUND, 1.0, ALU.add, ALU.max))
                v.memset(pair_end[:, 0:1], 0.0)
                then_read(v.tensor_tensor_scan(pair_end[:, 1:E + 1], one_row[:, 0:E], pairs[:, :], 0.0,
                                               ALU.mult, ALU.add))
                v.tensor_copy(first_pair[:, :], pair_end[:, :])
                then_read(v.scalar_tensor_tensor(out=pairs[:, :], in0=pair_end[:, 0:E], scalar=float(PAIR),
                                                 in1=before[:, :, 0], op0=ALU.mult, op1=ALU.subtract))
                then_read(v.tensor_tensor(base[:, :, :], before[:, :, :], psR[:, 0, 0:E * NT]
                                          .rearrange("p (e t) -> p e t", t=NT), ALU.add))
                then_read(v.scalar_tensor_tensor(out=base[:, :, :], in0=base[:, :, :], scalar=-1.0,
                                                 in1=pairs[:, :].unsqueeze(2).to_broadcast([P, E, NT]),
                                                 op0=ALU.add, op1=ALU.add))
                for k in range(TOP):
                    ins = v.tensor_tensor(picked[k][:, :, :], picked[k][:, :, :], base[:, :, :], ALU.mult)
                then_read(ins)
                for k in range(TOP):
                    ins = v.tensor_reduce(rows[:, k], picked[k][:, :, :].rearrange("p e t -> p t e"), AX.X, ALU.add)
                then_read(ins)
                for k in range(TOP):
                    v.tensor_copy(row_of[k][:, :], rows[:, k])
                then_read(v.tensor_scalar(tile_q[:, :, :], rows[:, :, :], 1.0 / P, 0.5 / P - 0.5, ALU.mult, ALU.add))
                then_read(v.tensor_scalar(tile_q[:, :, :], tile_q[:, :, :], ROUND, None, ALU.add))
                then_read(v.tensor_scalar(tile_q[:, :, :], tile_q[:, :, :], -ROUND, None, ALU.add))
                then_read(v.scalar_tensor_tensor(out=tile_r[:, :, :], in0=tile_q[:, :, :], scalar=-float(P),
                                                 in1=rows[:, :, :], op0=ALU.mult, op1=ALU.add))
                for n in range(NG):
                    if n >= 2:
                        dve.wait_ge(placed, n - 1)
                    for i in range(GROUP):
                        k, t = divmod(n * GROUP + i, NT)
                        v.tensor_scalar(hot_r[:, n % 2, i, :], iota_q[:, :], tile_r[:, k, t:t + 1], None,
                                        ALU.is_equal)
                        ins = v.tensor_scalar(hot_q[:, n % 2, i, :], iota_q[:, 0:NQ], tile_q[:, k, t:t + 1],
                                              token_id[:, t:t + 1], ALU.is_equal, ALU.mult)
                    ins.then_inc(hot, 1)
                dve.wait_ge(placed, NG)
                v.tensor_copy(token_of[:, :], psR[:, 2, 0:NQ])

        stage = ExitStack()
        with stage:
            def sb(name, shape, dt=F32):
                return stage.enter_context(nc.sbuf_tensor(name, shape, dt))

            def sem(name):
                return stage.enter_context(nc.semaphore(name))

            which = [sb(f"which{h}", [P, 1], U32) for h in range(HALVES)]
            tick = sb("tick", [P, 1])
            nothing = sb("b_nothing", [P, 16])
            xs = sb("xs", [P, HALVES, H])
            xsT = [sb(f"xsT_{p}", [P, KH, PAIR], F32R) for p in ("hi", "lo")]
            gate = sb("gate", [P, KI, PAIR])
            hid = sb("hid", [P, KI, PAIR])
            hidT = [sb(f"hidT_{p}", [P, KI, PAIR], F32R) for p in ("hi", "lo")]
            eo = sb("eo", [P, HALVES, H])
            psT = stage.enter_context(nc.psum_tensor("psT", [P, HALVES, 512], F32))
            psG = stage.enter_context(nc.psum_tensor("psG", [P, KI, 2, 256], F32))
            psO = stage.enter_context(nc.psum_tensor("psO", [P, HALVES, 512], F32))

            we_loaded = sem("we_loaded")
            we_hi = sem("we_hi")
            we_lo = sem("we_lo")
            we_lo_pool = sem("we_lo_pool")
            tick_made = sem("tick_made")
            which_done = sem("which_done")
            xs_loaded = [sem(f"xs{h}_loaded") for h in range(HALVES)]
            xsT_full = sem("xsT_full")
            xsT_hi = sem("xsT_hi")
            xsT_lo = sem("xsT_lo")
            gu_full = sem("gu_full")
            gate_done = sem("gate_done")
            hid_done = sem("hid_done")
            hid_hi = sem("hid_hi")
            hid_lo = sem("hid_lo")
            eo_full = sem("eo_full")
            eo_done = sem("eo_done")
            eo_stored = [sem(f"eo{h}_stored") for h in range(HALVES)]
            block = stage.enter_context(nc.Block())

            def start_of(e, i):
                return e.value_load(first_pair[0:1, bass.ds(i, 1)], min_val=0, max_val=MAX_PAIRS)

            def experts(e, each, tile_pair):
                with e.Fori(0, E // 2) as two:
                    for slot in range(2):
                        expert = two * 2 + slot
                        first, end = start_of(e, expert), start_of(e, expert + 1)
                        each(expert, slot)
                        with e.Fori(first, end) as pair:
                            tile_pair(pair, slot)

            @block.sync
            def _(sp):
                load_expert(sp, we_raw, 1, we_loaded)

                def each(expert, slot):
                    sp.wait_ge(we_lo, expert + 2)
                    sp.wait_ge(we_lo_pool, expert + 2)
                    load_expert(sp, we_raw, (expert + 2) % E, we_loaded)

                def tile_pair(pair, slot):
                    for h in range(HALVES):
                        sp.wait_ge(eo_done, pair * HALVES + h + 3)
                        sp.dma_start(eo_rows[pair * HALVES + h], eo[:, h, :]).then_inc(eo_stored[h], 16)

                experts(sp, each, tile_pair)
                sp.wait_ge(we_loaded, 64 * (E + 1))

            @block.gpsimd
            def _(pool):
                g = nc.gpsimd
                g.memset(tick[:, :], 0.0).then_inc(tick_made, 1)
                pool.wait_ge(tick_made, 1)
                g.memset(tick[:, :], 0.0).then_inc(we_lo_pool, 1)
                pool.wait_ge(we_lo_pool, 1)

                def fetch(pair):
                    for h in range(HALVES):
                        n = pair * HALVES + h
                        pool.wait_ge(xsT_full, n + 1)
                        g.tensor_copy(which[h][:, :], token_of[:, bass.ds(n, 1)]).then_inc(which_done, 1)
                        pool.wait_ge(which_done, n + 1)
                        g.tensor_tensor(tick[:, :], tick[:, :], tick[:, :], ALU.add)
                        g.indirect_dma_start(out=xs[:, h, :], out_offset=None, in_=xn_dram[:, :],
                                             in_offset=bass.IndirectOffsetOnAxis(ap=which[h][:, 0:1], axis=0)
                                             ).then_inc(xs_loaded[h], 16)

                def split(expert, slot):
                    pool.wait_ge(we_hi, expert * 2 + 2)
                    for rows, cols in WE_SHARES[1]:
                        ins = g.tensor_tensor(we[1 - slot][1][rows, cols], we_raw[rows, cols],
                                              we[1 - slot][0][rows, cols].bitcast(F32), ALU.subtract)
                    ins.then_inc(we_lo_pool, 1)

                for pair in range(FETCH_AHEAD):
                    fetch(pair)
                experts(pool, split, lambda pair, slot: fetch(pair + FETCH_AHEAD))
                n_pairs = start_of(pool, E)
                for h in range(HALVES):
                    pool.wait_ge(eo_stored[h], n_pairs * 16 + 16)
                    pool.wait_ge(xs_loaded[h], n_pairs * 16 + 16 * FETCH_AHEAD)

            @block.tensor
            def _(pe):
                t = nc.tensor

                def turn(pair, h):
                    pe.wait_ge(xs_loaded[h], pair * 16 + 16)
                    pe.wait_ge(xsT_lo, pair * HALVES + h + 1)
                    for k in range(KH):
                        ins = t.transpose(psT[:, h, k * P:(k + 1) * P], xs[:, h, k * P:(k + 1) * P], ident[:, :])
                    ins.then_inc(xsT_full, 1)

                def gate_up(pair, slot, j):
                    rows = k_rows(j)
                    pe.wait_ge(hid_done, pair * KI + j + 1)
                    for g in range(2):
                        m = 0
                        for k in range(KH):
                            c0 = (2 * k + g) * I + j * P
                            for a, c in PARTS:
                                ins = t.matmul(psG[0:rows, j, g, 0:PAIR], we[slot][a][:, c0:c0 + rows],
                                               xsT[c][:, k, :], start=(m == 0), stop=(m == 3 * KH - 1))
                                m += 1
                    ins.then_inc(gu_full, 1)

                def down(pair, slot, h):
                    pe.wait_ge(eo_done, pair * HALVES + h + 1)
                    m = 0
                    for k in range(KI):
                        rows = k_rows(k)
                        if h == 0:
                            pe.wait_ge(hid_lo, pair * KI + k + 1 + KI)
                        for a, c in PARTS:
                            ins = t.matmul(psO[:, h, :], hidT[a][0:rows, k, h * P:(h + 1) * P],
                                           we[slot][c][0:rows, GU + k * H:GU + (k + 1) * H],
                                           start=(m == 0), stop=(m == 3 * KI - 1))
                            m += 1
                    ins.then_inc(eo_full, 1)

                def tile_pair(pair, slot):
                    pe.wait_ge(xsT_lo, pair * HALVES + 4)
                    for j in range(KI):
                        gate_up(pair, slot, j)
                    for h in range(HALVES):
                        turn(pair + 1, h)
                    for h in range(HALVES):
                        down(pair, slot, h)

                for h in range(HALVES):
                    turn(0, h)

                def each(expert, slot):
                    pe.wait_ge(const_made, 6)
                    pe.wait_ge(we_lo, expert + 1)
                    pe.wait_ge(we_lo_pool, expert + 1)

                experts(pe, each, tile_pair)

            @block.scalar
            def _(act):
                s = nc.scalar

                def split(expert, slot):
                    act.wait_ge(we_loaded, expert * 64 + 64)
                    for share in WE_SHARES:
                        for rows, cols in share:
                            ins = s.activation(we[1 - slot][0][rows, cols], we_raw[rows, cols], ACT.Copy)
                        ins.then_inc(we_hi, 1)

                def turned(pair, h):
                    act.wait_ge(xsT_full, pair * HALVES + h + 3)
                    s.activation(xsT[0][:, :, h * P:(h + 1) * P], psT[:, h, :].rearrange("p (k n) -> p k n", n=P),
                                 ACT.Copy).then_inc(xsT_hi, 1)

                def silu(pair, j):
                    rows = k_rows(j)
                    act.wait_ge(gu_full, pair * KI + j + 1)
                    s.activation(gate[0:rows, j, :], psG[0:rows, j, 0, 0:PAIR], ACT.Silu).then_inc(gate_done, 1)

                def hidden(pair, j):
                    rows = k_rows(j)
                    act.wait_ge(hid_done, pair * KI + j + 1 + KI)
                    s.activation(hidT[0][0:rows, j, :], hid[0:rows, j, :], ACT.Copy).then_inc(hid_hi, 1)

                def output(pair, h):
                    act.wait_ge(eo_full, pair * HALVES + h + 1)
                    act.wait_ge(eo_stored[h], pair * 16 + 16)
                    s.activation(eo[:, h, :], psO[:, h, :], ACT.Copy).then_inc(eo_done, 1)

                def tile_pair(pair, slot):
                    silu(pair, 0)
                    for j in range(1, KI):
                        silu(pair, j)
                        hidden(pair, j - 1)
                    hidden(pair, KI - 1)
                    for h in range(HALVES):
                        turned(pair + 1, h)
                    for h in range(HALVES):
                        output(pair, h)

                for h in range(HALVES):
                    turned(0, h)
                experts(act, split, tile_pair)

            @block.vector
            def _(dve):
                v = nc.vector
                for n, (sm, by) in enumerate(((xsT_full, 2), (xsT_lo, 2), (hid_done, KI), (hid_lo, KI), (eo_done, 2),
                                              (eo_stored[0], 16), (eo_stored[1], 16), (we_lo, 1))):
                    v.memset(nothing[:, n:n + 1], 0.0).then_inc(sm, by)

                def split(expert, slot):
                    dve.wait_ge(we_hi, expert * 2 + 1)
                    for rows, cols in WE_SHARES[0]:
                        ins = v.tensor_tensor(we[1 - slot][1][rows, cols], we_raw[rows, cols],
                                              we[1 - slot][0][rows, cols].bitcast(F32), ALU.subtract)
                    ins.then_inc(we_lo, 1)

                def turned(pair, h):
                    dve.wait_ge(xsT_hi, pair * HALVES + h + 1)
                    cols = slice(h * P, (h + 1) * P)
                    v.tensor_tensor(xsT[1][:, :, cols], psT[:, h, :].rearrange("p (k n) -> p k n", n=P),
                                    xsT[0][:, :, cols].bitcast(F32), ALU.subtract).then_inc(xsT_lo, 1)

                def product(pair, j):
                    rows = k_rows(j)
                    dve.wait_ge(gate_done, pair * KI + j + 1)
                    dve.wait_ge(hid_lo, pair * KI + j + 1)
                    v.tensor_tensor(hid[0:rows, j, :], psG[0:rows, j, 1, 0:PAIR], gate[0:rows, j, :], ALU.mult
                                    ).then_inc(hid_done, 1)

                def hidden(pair, j):
                    rows = k_rows(j)
                    dve.wait_ge(hid_hi, pair * KI + j + 1)
                    v.tensor_tensor(hidT[1][0:rows, j, :], hid[0:rows, j, :], hidT[0][0:rows, j, :].bitcast(F32),
                                    ALU.subtract).then_inc(hid_lo, 1)

                def tile_pair(pair, slot):
                    product(pair, 0)
                    for j in range(1, KI):
                        product(pair, j)
                        hidden(pair, j - 1)
                    hidden(pair, KI - 1)
                    for h in range(HALVES):
                        turned(pair + 1, h)

                for h in range(HALVES):
                    turned(0, h)
                experts(dve, split, tile_pair)

        experts_weights.close()

        stage = ExitStack()
        with stage:
            def sb(name, shape, dt=F32):
                return stage.enter_context(nc.sbuf_tensor(name, shape, dt))

            def sem(name):
                return stage.enter_context(nc.semaphore(name))

            NJ = SL * KI
            wo = [sb(f"wo_{p}", [P, XT, H], F32R) for p in ("hi", "lo")]
            nw_col = sb("nw_col", [P, XT])
            xnrow = sb("c_xnrow", [P, C, H])
            xT = [sb(f"c_xT_{p}", [P, KH, L], F32R) for p in ("hi", "lo")]
            gate = sb("c_gate", [P, 2, L])
            hid = sb("c_hid", [P, 2, L])
            hidT = [sb(f"c_hidT_{p}", [P, NJ, L], F32R) for p in ("hi", "lo")]
            y_raw = sb("y_raw", [P, C, XT * P])
            yT = [sb(f"yT_{p}", [P, XT * P], F32R) for p in ("hi", "lo")]
            ysq = sb("ysq_c", [P, XT * P])
            yred = sb("yred_c", [P, 2, P])
            nwt = sb("c_nwt", [P, 3, C])
            y_scale = sb("y_scale", [P, C])
            room = sb("room", [P, XT, H])
            picked_rows = [[room[:, 2 * i + k, :] for k in range(TOP)] for i in range(2)]
            moe = [room[:, 4 + i, :] for i in range(2)]
            xrow = [room[:, 6 + i, :] for i in range(2)]
            which = [[sb(f"c_which{i}{k}", [P, 1], U32) for k in range(TOP)] for i in range(2)]
            tick = sb("c_tick", [P, 1])
            nothing = sb("c_nothing", [P, 16])
            assert XT == 8 and TOP == 2
            psT = stage.enter_context(nc.psum_tensor("c_psT", [P, 512], F32))
            psG = stage.enter_context(nc.psum_tensor("c_psG", [P, 2, 2, 512], F32))
            psM = stage.enter_context(nc.psum_tensor("psM", [P, 512], F32))
            psY = stage.enter_context(nc.psum_tensor("psY", [P, 512], F32))
            psQ = stage.enter_context(nc.psum_tensor("psQ", [P, C, P], F32))

            nw_loaded = sem("nw_loaded")
            wo_loaded = sem("wo_loaded")
            wo_scaled = sem("wo_scaled")
            wo_hi = sem("wo_hi")
            wo_lo = sem("wo_lo")
            xn_loaded = sem("c_xn_loaded")
            x_loaded = [sem(f"c_x{i}_loaded") for i in range(2)]
            y_loaded = [sem(f"y{t}_loaded") for t in range(C)]
            rows_loaded = [[sem(f"rows{i}{k}_loaded") for k in range(TOP)] for i in range(2)]
            tick_made = sem("c_tick_made")
            which_done = sem("c_which_done")
            xT_full = sem("c_xT_full")
            xT_hi = sem("c_xT_hi")
            xT_lo = sem("c_xT_lo")
            gu_full = sem("c_gu_full")
            gate_done = sem("c_gate_done")
            hid_done = sem("c_hid_done")
            hid_hi = sem("c_hid_hi")
            hid_lo = sem("c_hid_lo")
            ysq_done = sem("ysq_done")
            yred_done = sem("yred_done")
            sq_full = sem("sq_full")
            sq_read = sem("sq_read")
            yT_hi = sem("yT_hi")
            yT_lo = sem("yT_lo")
            mix_full = sem("mix_full")
            moe_full = sem("moe_full")
            first_done = sem("first_done")
            moe_done = sem("moe_done")
            silu_done = sem("silu_done")
            mix_done = sem("mix_done")
            res_done = sem("res_done")
            res_stored = [sem(f"res{i}_stored") for i in range(2)]
            own = sem("c_own")
            block = stage.enter_context(nc.Block())
            xn_tok_c = xn_dram.rearrange("(b c p) h -> b p c h", b=B, p=P)
            OWN = 14

            def x_tile(dram, b, t):
                return dram.rearrange("b (c p) h -> b c p h", p=P)[b, t]

            @block.sync
            def _(sp):
                with nc.allow_non_contiguous_dma(reason="a small parameter"):
                    sp.dma_start(nw_col[:, :], norm_w.rearrange("(t p) -> p t", p=P)).then_inc(nw_loaded, 16)
                sp.dma_start(xnrow[:, :, :], xn_tok_c[0]).then_inc(xn_loaded, 16)
                for t in range(C):
                    sp.dma_start(y_raw[:, t, :], y_dram[0, t]).then_inc(y_loaded[t], 16)
                sp.dma_start(room[:, :, :], W_out.rearrange("(k p) n -> p k n", p=P)
                             ).then_inc(wo_loaded, 16)
                sp.wait_ge(wo_lo, 1)
                for t in range(2):
                    sp.dma_start(xrow[t], x_tile(x, 0, t)).then_inc(x_loaded[t], 16)
                with sp.Fori(0, B) as b:
                    after_b = (b + 1) % B
                    sp.wait_ge(xT_full, b * KH + KH)
                    sp.dma_start(xnrow[:, :, :], xn_tok_c[after_b]).then_inc(xn_loaded, 16)
                    for t in range(C):
                        sp.wait_ge(yT_lo, b * C + t + 1)
                        sp.dma_start(y_raw[:, t, :], y_dram[after_b, t]).then_inc(y_loaded[t], 16)
                        sp.wait_ge(res_done, b * C + t + 3)
                        sp.dma_start(x_tile(out, b, t), xrow[t % 2]).then_inc(res_stored[t % 2], 16)
                        sp.wait_ge(res_stored[t % 2], b * 16 * (C // 2) + 16 * (t // 2) + 32)
                        if t + 2 < C:
                            src = x_tile(x, b, t + 2)
                        else:
                            src = x_tile(x, after_b, t + 2 - C)
                        sp.dma_start(xrow[t % 2], src).then_inc(x_loaded[t % 2], 16)
                for i in range(2):
                    sp.wait_ge(x_loaded[i], 16 * (B * C // 2 + 1))
                for t in range(C):
                    sp.wait_ge(y_loaded[t], 16 * (B + 1))
                sp.wait_ge(xn_loaded, 16 * (B + 1))

            @block.gpsimd
            def _(pool):
                g = nc.gpsimd
                g.memset(tick[:, :], 0.0).then_inc(tick_made, 1)
                pool.wait_ge(tick_made, 1)
                pool.wait_ge(wo_lo, 1)
                with pool.Fori(0, NT // 2) as two:
                    for i in range(2):
                        n = two * 2 + i
                        pool.wait_ge(moe_done, n + 1)
                        for k in range(TOP):
                            g.tensor_copy(which[i][k][:, :], row_of[k][:, bass.ds(n, 1)]).then_inc(which_done, 1)
                        pool.wait_ge(which_done, n * TOP + TOP)
                        g.tensor_tensor(tick[:, :], tick[:, :], tick[:, :], ALU.add)
                        for k in range(TOP):
                            g.indirect_dma_start(out=picked_rows[i][k], out_offset=None,
                                                 in_=eo_dram[:, :],
                                                 in_offset=bass.IndirectOffsetOnAxis(ap=which[i][k][:, 0:1], axis=0)
                                                 ).then_inc(rows_loaded[i][k], 16)

            @block.tensor
            def _(pe):
                te = nc.tensor

                def turn(n, k):
                    pe.wait_ge(xT_lo, n + 1)
                    for c in range(C):
                        ins = te.transpose(psT[:, c * P:(c + 1) * P], xnrow[:, c, k * P:(k + 1) * P], ident[:, :])
                    ins.then_inc(xT_full, 1)

                pe.wait_ge(xn_loaded, 16)
                for k in range(KH):
                    turn(k, k)
                with pe.Fori(0, B) as b:
                    pe.wait_ge(xT_lo, b * KH + KH + 1)
                    for j in range(NJ):
                        n, kt = divmod(j, KI)
                        rows = k_rows(kt)
                        pe.wait_ge(hid_done, b * NJ + j + 1)
                        for g in range(2):
                            m = 0
                            for k in range(KH):
                                c0 = (2 * k + g) * I + kt * P
                                for a, c in PARTS:
                                    ins = te.matmul(psG[0:rows, j % 2, g, :], ws[a][:, n, c0:c0 + rows],
                                                    xT[c][:, k, :], start=(m == 0), stop=(m == 3 * KH - 1))
                                    m += 1
                        ins.then_inc(gu_full, 1)
                        if 1 <= j <= C:
                            t = j - 1
                            pe.wait_ge(yred_done, b * C + t + 2)
                            pe.wait_ge(sq_read, b + 1)
                            te.matmul(psQ[:, t, :], yred[:, t % 2, :], ones[:, :], start=True, stop=True
                                      ).then_inc(sq_full, 1)
                    def mixer(t):
                        i = b * C + t
                        if t == 0:
                            pe.wait_ge(wo_lo, 1)
                        pe.wait_ge(yT_lo, i + 1)
                        pe.wait_ge(mix_done, i + 1)
                        m = 0
                        for k in range(XT):
                            for a, c in PARTS:
                                ins = te.matmul(psY[:, :], yT[a][:, k * P:(k + 1) * P], wo[c][:, k, :],
                                                start=(m == 0), stop=(m == 3 * XT - 1))
                                m += 1
                        ins.then_inc(mix_full, 1)

                    def down(t):
                        pe.wait_ge(first_done, b * C + t + 1)
                        m = 0
                        for j in range(NJ):
                            n, kt = divmod(j, KI)
                            rows = k_rows(kt)
                            if t == 0:
                                pe.wait_ge(hid_lo, b * NJ + j + 3)
                            for a, c in PARTS:
                                ins = te.matmul(psM[:, :], hidT[a][0:rows, j, t * P:(t + 1) * P],
                                                ws[c][0:rows, n, GU + kt * H:GU + (kt + 1) * H],
                                                start=(m == 0), stop=(m == 3 * NJ - 1))
                                m += 1
                        ins.then_inc(moe_full, 1)

                    mixer(0)
                    down(0)
                    for t in range(C):
                        if t:
                            down(t)
                        else:
                            pe.wait_ge(xn_loaded, b * 16 + 32)
                        turn(b * KH + KH + t, t)
                        if t:
                            mixer(t)

            @block.scalar
            def _(act):
                s = nc.scalar

                def turned(n, k):
                    act.wait_ge(xT_full, n + 1)
                    s.activation(xT[0][:, k, :], psT[:, :], ACT.Copy).then_inc(xT_hi, 1)

                for k in range(KH):
                    turned(k, k)

                act.wait_ge(wo_loaded, 16)
                act.wait_ge(nw_loaded, 16)
                for k in range(XT):
                    ins = s.activation(room[:, k, :], room[:, k, :], ACT.Copy,
                                       scale=nw_col[:, k:k + 1])
                ins.then_inc(wo_scaled, 1)
                act.wait_ge(wo_scaled, 1)
                s.activation(wo[0][:, :, :], room[:, :, :], ACT.Copy).then_inc(wo_hi, 1)

                with act.Fori(0, B) as b:
                    def silu(j):
                        act.wait_ge(gu_full, b * NJ + j + 1)
                        rows = k_rows(j % KI)
                        s.activation(gate[0:rows, j % 2, :], psG[0:rows, j % 2, 0, :], ACT.Silu
                                     ).then_inc(gate_done, 1)

                    def hidden(j):
                        act.wait_ge(hid_done, b * NJ + j + 3)
                        rows = k_rows(j % KI)
                        s.activation(hidT[0][0:rows, j, :], hid[0:rows, j % 2, :], ACT.Copy).then_inc(hid_hi, 1)

                    def square(t):
                        act.wait_ge(y_loaded[t], b * 16 + 16)
                        act.wait_ge(yred_done, b * C + t + 1)
                        s.activation(ysq[:, :], y_raw[:, t, :], ACT.Square).then_inc(ysq_done, 1)

                    def split_y(t):
                        act.wait_ge(mix_full, b * C + t + 1)
                        s.activation(yT[0][:, :], y_raw[:, t, :], ACT.Copy).then_inc(yT_hi, 1)

                    for j in range(NJ):
                        if j < C:
                            square(j)
                        silu(j)
                        if j:
                            hidden(j - 1)
                        if j == C:
                            split_y(0)
                    hidden(NJ - 1)
                    split_y(1)
                    for t in range(C):
                        turned(b * KH + KH + t, t)
                        act.wait_ge(moe_done, b * C + t + 3)
                        s.activation(moe[t % 2], moe[t % 2], ACT.Silu).then_inc(silu_done, 1)
                        if 0 < t < C - 1:
                            split_y(t + 1)

            @block.vector
            def _(dve):
                v = nc.vector
                for n, (sm, by) in enumerate(((xT_lo, 1), (hid_done, 2), (hid_lo, 2), (yred_done, 1), (sq_full, 2),
                                              (sq_read, 1), (mix_full, 1), (first_done, 1), (moe_done, 2),
                                              (mix_done, 1), (res_done, 2), (res_stored[0], 16),
                                              (res_stored[1], 16))):
                    v.memset(nothing[:, n:n + 1], 0.0).then_inc(sm, by)

                def turned(n, k):
                    dve.wait_ge(xT_hi, n + 1)
                    v.tensor_tensor(xT[1][:, k, :], psT[:, :], xT[0][:, k, :].bitcast(F32), ALU.subtract
                                    ).then_inc(xT_lo, 1)

                for k in range(KH):
                    turned(k, k)
                dve.wait_ge(wo_hi, 1)
                v.tensor_tensor(wo[1][:, :, :], room[:, :, :], wo[0][:, :, :].bitcast(F32),
                                ALU.subtract).then_inc(wo_lo, 1)

                with dve.Fori(0, B) as b:
                    n_own = [0]

                    def then_read(ins):
                        n_own[0] += 1
                        ins.then_inc(own, 1)
                        dve.wait_ge(own, b * OWN + n_own[0])

                    def product(j):
                        rows = k_rows(j % KI)
                        dve.wait_ge(gate_done, b * NJ + j + 1)
                        dve.wait_ge(hid_lo, b * NJ + j + 1)
                        v.tensor_tensor(hid[0:rows, j % 2, :], psG[0:rows, j % 2, 1, :], gate[0:rows, j % 2, :],
                                        ALU.mult).then_inc(hid_done, 1)

                    def hidden(j):
                        rows = k_rows(j % KI)
                        dve.wait_ge(hid_hi, b * NJ + j + 1)
                        v.tensor_tensor(hidT[1][0:rows, j, :], hid[0:rows, j % 2, :],
                                        hidT[0][0:rows, j, :].bitcast(F32), ALU.subtract).then_inc(hid_lo, 1)

                    def reduce_squares(t):
                        dve.wait_ge(ysq_done, b * C + t + 1)
                        dve.wait_ge(sq_full, b * C + t + 1)
                        v.tensor_reduce(yred[:, t % 2, :], ysq[:, :].rearrange("p (j l) -> p l j", l=P), AX.X,
                                        ALU.add).then_inc(yred_done, 1)

                    def split_y(t):
                        dve.wait_ge(yT_hi, b * C + t + 1)
                        v.tensor_tensor(yT[1][:, :], y_raw[:, t, :], yT[0][:, :].bitcast(F32), ALU.subtract
                                        ).then_inc(yT_lo, 1)

                    for j in range(NJ):
                        if j < C:
                            reduce_squares(j)
                        product(j)
                        if j:
                            hidden(j - 1)
                        if j == C:
                            split_y(0)
                    hidden(NJ - 1)
                    dve.wait_ge(sq_full, b * C + C + 2)
                    v0, v1, v2 = (nwt[:, i, :] for i in range(3))
                    v.tensor_scalar(v0, psQ[:, :, 0], 1.0 / INNER, 1e-5, ALU.mult, ALU.add).then_inc(sq_read, 1)
                    dve.wait_ge(sq_read, b + 2)
                    dve.wait_ge(mix_done, b * C + 1)
                    then_read(v.tensor_scalar(y_scale[:, :].bitcast(I32), v0.bitcast(I32), -0.5, 1597463007.0,
                                              ALU.mult, ALU.add))
                    for _ in range(4):
                        then_read(v.tensor_tensor(v1, y_scale[:, :], y_scale[:, :], ALU.mult))
                        then_read(v.scalar_tensor_tensor(out=v2, in0=v1, scalar=-0.5, in1=v0, op0=ALU.mult,
                                                         op1=ALU.mult))
                        then_read(v.scalar_tensor_tensor(out=y_scale[:, :], in0=v2, scalar=1.5, in1=y_scale[:, :],
                                                         op0=ALU.add, op1=ALU.mult))
                    for t in range(C):
                        i = b * C + t
                        if t == 0:
                            split_y(1)
                        half = b * 16 * (C // 2) + 16 * (t // 2) + 16
                        m = moe[t % 2]
                        dve.wait_ge(moe_full, i + 1)
                        dve.wait_ge(rows_loaded[t % 2][0], half)
                        dve.wait_ge(res_done, i + 1)
                        v.scalar_tensor_tensor(out=m, in0=picked_rows[t % 2][0],
                                               scalar=weight[0][:, bass.ds(i, 1)], in1=psM[:, :],
                                               op0=ALU.mult, op1=ALU.add).then_inc(first_done, 1)
                        dve.wait_ge(first_done, i + 2)
                        dve.wait_ge(rows_loaded[t % 2][1], half)
                        v.scalar_tensor_tensor(out=m, in0=picked_rows[t % 2][1],
                                               scalar=weight[1][:, bass.ds(i, 1)], in1=m,
                                               op0=ALU.mult, op1=ALU.add).then_inc(moe_done, 1)
                        turned(b * KH + KH + t, t)
                        dve.wait_ge(silu_done, i + 1)
                        dve.wait_ge(mix_full, i + 2)
                        if t == 0:
                            then_read(v.memset(nothing[:, 15:16], 0.0))
                        v.scalar_tensor_tensor(out=m, in0=psY[:, :], scalar=y_scale[:, t:t + 1],
                                               in1=m, op0=ALU.mult, op1=ALU.mult).then_inc(mix_done, 1)
                        if 0 < t < C - 1:
                            split_y(t + 1)
                        dve.wait_ge(mix_done, i + 2)
                        dve.wait_ge(x_loaded[t % 2], half)
                        v.tensor_tensor(xrow[t % 2], m, xrow[t % 2], ALU.add).then_inc(res_done, 1)
                    assert n_own[0] == OWN, n_own[0]


_INPUTS = ["hidden_states", "W_in", "conv_w", "conv_b", "A", "D", "dt_bias", "norm_w", "W_out"]
_FFN = ["gate_w", "w_gate", "w_up", "w_down", "sw_gate", "sw_up", "sw_down"]


def kernel(**inputs):
    import numpy as np
    import concourse.bacc as bacc
    from concourse.bass_utils import run_bass_kernel_spmd

    names = ["L0_attn_" + n for n in _INPUTS] + ["L0_ffn_" + n for n in _FFN]
    nc = bacc.Bacc("TRN2", target_bir_lowering=False, num_devices=1)
    arrays, args = {}, []
    for name in names:
        a = np.ascontiguousarray(inputs[name])
        arrays[name + "_dram"] = a
        args.append(nc.dram_tensor(name + "_dram", a.shape, mybir.dt.from_np(a.dtype), kind="ExternalInput").ap())
    out = nc.dram_tensor("out_dram", inputs["L0_attn_hidden_states"].shape, F32, kind="ExternalOutput").ap()
    program(nc, *args, out)
    result = run_bass_kernel_spmd(nc, [arrays], core_ids=[0])
    return result.results[0]["out_dram"]
```

```python
from contextlib import ExitStack

import concourse.bass as bass
from concourse import mybir

F32 = mybir.dt.float32
F32R = mybir.dt.float32r
U32 = mybir.dt.uint32
I32 = mybir.dt.int32
ALU = mybir.AluOpType
ACT = mybir.ActivationFunctionType
AX = mybir.AxisListType

P = 128
PARTS = ((0, 0), (0, 1), (1, 0))


class Ring:

    def __init__(self, uses, slots):
        self.at = {}
        self.per_slot = [0] * slots
        for n, name in enumerate(uses):
            self.at[name] = (n % slots, self.per_slot[n % slots])
            self.per_slot[n % slots] += 1


def program(nc, x, W_in, conv_w, conv_b, A, D, dt_bias, norm_w, W_out, gate_w, w_gate, w_up, w_down,
            sw_gate, sw_up, sw_down, out):
    B, L, H = x.shape
    N = B * L
    KH = H // P
    CONV, TAPS = conv_w.shape
    NHEADS = A.shape[0]
    INNER = norm_w.shape[0]
    HD = INNER // NHEADS
    STATE = (CONV - INNER) // 2
    E, _, I = w_gate.shape
    IS = sw_gate.shape[1]
    ZT, CT = INNER // P, CONV // P
    XT = INNER // P
    C = L // P
    NT = N // P
    HH = NHEADS // 2
    assert STATE == P and L == 512 and H == 512 and NHEADS + E <= P

    TOP = 2
    HALVES = 2
    PAIR = HALVES * P
    MIN_PAIRS = TOP * N // PAIR
    MAX_PAIRS = MIN_PAIRS + E - 1
    FETCH_AHEAD = 2
    NQ = HALVES * (MAX_PAIRS + FETCH_AHEAD)
    assert NQ <= P and TOP == 2

    y_dram = nc.dram_tensor("mixer_y", (B, C, P, XT * P), F32).ap()
    xn_dram = nc.dram_tensor("xn_rows", (N, H), F32).ap()

    eo_dram = nc.dram_tensor("expert_rows", (MAX_PAIRS * PAIR, H), F32).ap()
    eo_rows = eo_dram.rearrange("(t p) h -> t p h", p=P)

    x_tok = x.rearrange("b (c p) h -> b p c h", p=P)
    xn_tok = xn_dram.rearrange("(b c p) h -> b p c h", b=B, p=P)

    outer = ExitStack()
    with outer:
        def keep(name, shape, dt=F32):
            return outer.enter_context(nc.sbuf_tensor(name, shape, dt))

        ident = keep("ident", [P, P])
        upto = keep("upto", [P, P])
        after = keep("after", [P, P])
        ones = keep("ones", [P, P])
        logits = keep("logits", [P, NT, E])
        choice = keep("choice", [P, 2, NT])
        top = keep("top", [P, NT])
        const_made = outer.enter_context(nc.semaphore("const_made"))
        y_stored = [outer.enter_context(nc.semaphore(f"y{i}_stored")) for i in range(2)]

        stage = ExitStack()
        with stage:
            def sb(name, shape, dt=F32):
                return stage.enter_context(nc.sbuf_tensor(name, shape, dt))

            def sem(name):
                return stage.enter_context(nc.semaphore(name))

            w_part = [sb(f"w_in_{p}", [P, KH, INNER + CONV], F32R) for p in ("hi", "lo")]
            DL = 32
            w_dtg = sb("w_dtg", [P, KH, P], F32R)
            assert NHEADS + E <= DL
            dtg_raw = sb("dtg_raw", [P, KH, P])
            after_r = sb("after_r", [P, P], F32R)
            cw = sb("cw", [P, CT, TAPS])
            cb = sb("cb", [P, CT])
            d_col = sb("d_col", [P, XT])
            a_row = sb("a_row", [P, NHEADS])
            bias_row = sb("bias_row", [P, NHEADS])
            xrow = sb("xrow", [P, C, H])
            xnT = [sb(f"xnT_{p}", [P, KH, L], F32R) for p in ("hi", "lo")]
            stats = sb("stats", [P, C, 6])
            mv = sb("mv", [P, C, 2])
            rstd = sb("rstd", [P, C])
            nwt = sb("nwt", [P, 3, C])
            acc = sb("acc", [P, 2, 2, L])
            xD = acc[:, 0].rearrange("p i l -> p (i l)").rearrange("p (j l) -> p j l", l=P)
            assert 2 * L == XT * P
            xbc = sb("xbc", [P, CT, L])
            zs = sb("zs", [P, ZT, L])
            dtgT = sb("dtgT", [P, L])
            dt_, dA, dA_lo, dt_in, u, w1, ln_w, tmp = [
                sb(n, [P, C, NHEADS]) for n in ("dt", "dA", "dA_lo", "dt_in", "u", "w1", "ln_w", "dt_tmp")]
            dA_hi = sb("dA_hi", [P, C, NHEADS], F32R)
            nothing = sb("nothing", [P, 8])
            logits_b = sb("logits_b", [P, C, E])
            best_b = sb("best_b", [P, C, 8])
            best_at_b = sb("best_at_b", [P, C, 8], U32)
            ex = sb("ex", [P, 3, C, NHEADS])
            seg_rhs = [sb(f"seg_rhs_{p}", [P, 2, HH, P], F32R) for p in ("hi", "lo")]
            decay = sb("decay", [P, 2, HH, P])
            cbm = sb("cbm", [P, P])
            btok = sb("btok", [P, P])
            xdt = sb("xdt", [P, INNER])
            xdec = sb("xdec", [P, INNER])
            state = sb("state", [P, INNER])
            yoff = sb("yoff", [P, INNER])
            ybuf = sb("ybuf", [P, 2, XT, P])

            psS = stage.enter_context(nc.psum_tensor("psS", [P, 2, 512], F32))
            psD = stage.enter_context(nc.psum_tensor("psD", [P, 3, 1024], F32))
            full = {k: [sem(f"ps{k}{i}_full") for i in range(n)] for k, n in (("S", 2), ("D", 3))}
            taken = {k: [sem(f"ps{k}{i}_taken") for i in range(n)] for k, n in (("S", 2), ("D", 3))}

            uses = {"S": ["dtg", "dtt", "sums"], "D": []}
            PAIRS = (ZT + CT) // 2
            FRONT_AT = PAIRS - 2

            def front(c):
                uses["S"].append(f"cb{c}")
                uses["D"].extend([f"xt{c}", f"seg{c}0", f"seg{c}1"])

            for j in range(PAIRS):
                if j == FRONT_AT:
                    front(0)
                uses["D"].append(f"p{j}")
            for c in range(C):
                if c:
                    uses["D"].append(f"off{c}")
                if c + 1 < C:
                    uses["D"].append(f"new{c}")
                uses["D"].append(f"y{c}")
                if c + 1 < C:
                    front(c + 1)
                uses["S"].append(f"xn{c}")
            rings = {"S": Ring(uses["S"], 2), "D": Ring(uses["D"], 3)}
            where = {n: (k, *v) for k, r in rings.items() for n, v in r.at.items()}
            if sum(len(r.at) for r in rings.values()) != len(where):
                raise ValueError("a PSUM use is named twice")

            param_loaded = sem("param_loaded")
            dtg_loaded = sem("dtg_loaded")
            STAGED = 4
            w_loaded = [sem(f"w{i}_loaded") for i in range(STAGED)]
            zeros_made = sem("zeros_made")
            rows_zeroed = sem("rows_zeroed")
            w_hi = sem("w_hi")
            w_lo = sem("w_lo")
            x_loaded = sem("x_loaded")
            xn_stored = sem("xn_stored")
            ln_done = sem("ln_done")
            xn0_full = sem("xn0_full")
            xnT_hi = sem("xnT_hi")
            xnT_lo = sem("xnT_lo")
            tap3 = sem("tap3")
            xbc_done = sem("xbc_done")
            dt_neg = sem("dt_neg")
            dt_exp = sem("dt_exp")
            dt_one = sem("dt_one")
            dt_ln = sem("dt_ln")
            dA_done = sem("dA_done")
            seg_hi = sem("seg_hi")
            seg_lo = sem("seg_lo")
            cbm_done = sem("cbm_done")
            m_done = sem("m_done")
            xdec_done = sem("xdec_done")
            xD_done = sem("xD_done")
            state_scaled = sem("state_scaled")
            y_done = sem("y_done")
            own = sem("own")

            XP = CT // 2
            OWN = 36
            NPARAM = 4 + P // HD
            WC = 288
            NW = (INNER + CONV) // WC
            assert STAGED * KH * WC <= CT * L
            w_raw = [xbc[:, :, :].rearrange("p t l -> p (t l)")[:, i * KH * WC:(i + 1) * KH * WC]
                     .rearrange("p (k n) -> p k n", k=KH) for i in range(STAGED)]
            w_cols = W_in.rearrange("(k p) n -> p k n", p=P)
            W_ORDER = [*range(INNER // WC, NW), *range(INNER // WC)]

            def w_slice(n):
                return slice(W_ORDER[n] * WC, (W_ORDER[n] + 1) * WC)

            def w_needed(end):
                return 3 + max(W_ORDER.index((end - 1) // WC), W_ORDER.index((end - 2 * P) // WC))

            def ps(name):
                k, slot, _ = where[name]
                return (psS if k == "S" else psD)[:, slot, :]

            def is_full(name):
                k, slot, _ = where[name]
                return full[k][slot]

            def is_taken(name):
                k, slot, _ = where[name]
                return taken[k][slot]

            def wait_full(e, b, name):
                k, slot, n = where[name]
                e.wait_ge(full[k][slot], b * rings[k].per_slot[slot] + n + 1)

            def wait_room(e, b, name):
                k, slot, n = where[name]
                e.wait_ge(taken[k][slot], b * rings[k].per_slot[slot] + n + 1)

            def wait_taken(e, b, name):
                k, slot, n = where[name]
                e.wait_ge(taken[k][slot], b * rings[k].per_slot[slot] + n + 2)

            def by_head(row, n=HD):
                return row.unsqueeze(2).to_broadcast([P, row.shape[1], n])

            def heads(flat):
                return flat.rearrange("p (h d) -> p h d", d=HD)

            block = stage.enter_context(nc.Block())

            @block.gpsimd
            def _(pool):
                g = nc.gpsimd
                g.memset(ident[:, :], 0.0).then_inc(const_made, 1)
                g.memset(ones[:, :], 1.0).then_inc(const_made, 1)
                g.memset(dtg_raw[:, :, :], 0.0).then_inc(const_made, 1)
                g.memset(zs[:, :, :], 0.0).then_inc(zeros_made, 1)
                pool.wait_ge(const_made, 3)
                g.affine_select(out=ident[:, :], in_=ident[:, :], compare_op=ALU.not_equal, fill=1.0,
                                base=0, pattern=[[-1, P]], channel_multiplier=1).then_inc(const_made, 1)
                g.affine_select(out=upto[:, :], in_=ones[:, :], compare_op=ALU.is_ge, fill=0.0,
                                base=0, pattern=[[1, P]], channel_multiplier=-1).then_inc(const_made, 1)
                g.affine_select(out=after[:, :], in_=ones[:, :], compare_op=ALU.is_gt, fill=0.0,
                                base=0, pattern=[[-1, P]], channel_multiplier=1).then_inc(const_made, 1)
                pool.wait_ge(const_made, 6)
                pool.wait_ge(param_loaded, 16 * NPARAM)

                with pool.Fori(0, B) as b:
                    pool.wait_ge(dA_done, b + 1)

                    def masked(c):
                        for half in range(2):
                            if c:
                                wait_full(pool, b, f"seg{c - 1}{half}")
                            hs = slice(half * HH, (half + 1) * HH)
                            g.tensor_tensor(seg_rhs[0][:, half], upto[:, :].unsqueeze(1).to_broadcast([P, HH, P]),
                                            by_head(dA_hi[:, c, hs].bitcast(F32), P), ALU.mult).then_inc(seg_hi, 1)

                    def skip(c):
                        if c:
                            wait_taken(pool, b, f"y{c - 1}")
                        else:
                            pool.wait_ge(xbc_done, b * XP + XP)
                        g.tensor_tensor(xD[:, :, :], xbc[:, 0:XT, c * P:(c + 1) * P],
                                        d_col[:, :].unsqueeze(2).to_broadcast([P, XT, P]),
                                        ALU.mult).then_inc(xD_done, 1)

                    masked(0)
                    skip(0)
                    for c in range(C - 1):
                        if c == 0:
                            wait_taken(pool, b, "sums")
                        else:
                            wait_full(pool, b, f"new{c - 1}")
                        wait_taken(pool, b, f"xt{c}")
                        g.tensor_tensor(heads(xdec[:, :]), heads(xdt[:, :]), by_head(ex[:, 1, c]),
                                        ALU.mult).then_inc(xdec_done, 1)
                        if c:
                            wait_full(pool, b, f"off{c}")
                            g.tensor_tensor(heads(state[:, :]), heads(state[:, :]), by_head(ex[:, 2, c]),
                                            ALU.mult).then_inc(state_scaled, 1)
                        masked(c + 1)
                        skip(c + 1)

            @block.sync
            def _(sp):
                with nc.allow_non_contiguous_dma(reason="small parameter tables"):
                    sp.dma_start(xrow[:, :, :], x_tok[0]).then_inc(x_loaded, 16)
                    for n in range(STAGED):
                        sp.dma_start(w_raw[n], w_cols[:, :, w_slice(n)]).then_inc(w_loaded[n], 16)
                for n in range(STAGED, NW):
                    sp.wait_ge(w_lo, n - STAGED + 3)
                    sp.dma_start(w_raw[n % STAGED], w_cols[:, :, w_slice(n)]).then_inc(w_loaded[n % STAGED], 16)

                sp.wait_ge(zeros_made, 1)
                spare = eo_dram[MIN_PAIRS * PAIR:, :].rearrange("(a p r) n -> a p (r n)", a=2, p=P)
                for n in range(2):
                    sp.dma_start(spare[n], zs[:, :, :].rearrange("p t l -> p (t l)")[:, 0:spare.shape[2]]
                                 ).then_inc(rows_zeroed, 16)

                with sp.Fori(0, B) as b:
                    sp.wait_ge(ln_done, b + 1)
                    sp.dma_start(xn_tok[b], xrow[:, :, :]).then_inc(xn_stored, 16)
                    sp.wait_ge(xn_stored, b * 16 + 16)
                    sp.wait_ge(xnT_lo, b * KH + KH)
                    sp.dma_start(xrow[:, :, :], x_tok[(b + 1) % B]).then_inc(x_loaded, 16)
                    for c in range(C):
                        sp.wait_ge(y_done, b * C + c + 1)
                        sp.dma_start(y_dram[b, c], ybuf[:, c % 2].rearrange("p j l -> p (j l)")
                                     ).then_inc(y_stored[c % 2], 16)

            @block.tensor
            def _(pe):
                t = nc.tensor

                def project(dst, w, j):
                    n = 0
                    for k in range(KH):
                        for s, m in PARTS:
                            ins = t.matmul(dst, w[s][:, k, j * P:(j + 1) * P], xnT[m][:, k, :],
                                           start=(n == 0), stop=(n == 3 * KH - 1))
                            n += 1
                    return ins

                def turn_x(dst, k):
                    for c in range(C):
                        ins = t.transpose(dst[:, c * P:(c + 1) * P], xrow[:, c, k * P:(k + 1) * P], ident[:, :])
                    return ins

                pe.wait_ge(const_made, 6)
                pe.wait_ge(ln_done, 1)
                for k in range(KH):
                    if k >= 2:
                        pe.wait_ge(xnT_lo, k - 1)
                    turn_x(psS[:, k % 2, :], k).then_inc(xn0_full, 1)
                pe.wait_ge(w_lo, 2)

                with pe.Fori(0, B) as b:
                    def front(c):
                        cols = slice(c * P, (c + 1) * P)
                        if c == 0:
                            pe.wait_ge(xbc_done, b * XP + XP)
                        wait_room(pe, b, f"cb{c}")
                        t.matmul(ps(f"cb{c}")[:, 0:P], xbc[:, XT, cols], xbc[:, XT + 1, cols],
                                 start=True, stop=True)
                        t.transpose(ps(f"cb{c}")[:, P:2 * P], xbc[:, XT, cols], ident[:, :]
                                    ).then_inc(is_full(f"cb{c}"), 1)
                        wait_room(pe, b, f"xt{c}")
                        for j in range(XT):
                            ins = t.transpose(ps(f"xt{c}")[:, j * P:(j + 1) * P], xbc[:, j, cols], ident[:, :])
                        ins.then_inc(is_full(f"xt{c}"), 1)
                        for half in range(2):
                            name = f"seg{c}{half}"
                            wait_room(pe, b, name)
                            pe.wait_ge(seg_hi, b * 2 * C + 2 * c + half + 1)
                            pe.wait_ge(seg_lo, b * 2 * C + 2 * c + half + 1)
                            for q in range(2):
                                hs = slice(q * HH // 2, (q + 1) * HH // 2)
                                for part in range(2):
                                    ins = t.matmul(ps(name)[:, q * 512:(q + 1) * 512], after_r[:, :],
                                                   seg_rhs[part][:, half, hs, :].rearrange("p h l -> p (h l)"),
                                                   start=(part == 0), stop=(part == 1))
                            ins.then_inc(is_full(name), 1)

                    def turn_next(c):
                        if c == 0:
                            pe.wait_ge(ln_done, b + 2)
                        wait_room(pe, b, f"xn{c}")
                        turn_x(ps(f"xn{c}"), c).then_inc(is_full(f"xn{c}"), 1)

                    pe.wait_ge(xnT_lo, b * KH + KH)
                    wait_room(pe, b, "dtg")
                    n = 0
                    for k in range(KH):
                        for m in range(2):
                            ins = t.matmul(ps("dtg"), w_dtg[:, k, :], xnT[m][:, k, :],
                                           start=(n == 0), stop=(n == 2 * KH - 1))
                            n += 1
                    ins.then_inc(is_full("dtg"), 1)
                    for j in range(PAIRS):
                        if j == FRONT_AT:
                            front(0)
                        first = ZT + 2 * j if j < XP else 2 * (j - XP)
                        wait_room(pe, b, f"p{j}")
                        pe.wait_ge(w_lo, w_needed((first + 2) * P))
                        for i in range(2):
                            ins = project(ps(f"p{j}")[:, i * L:(i + 1) * L], w_part, first + i)
                        ins.then_inc(is_full(f"p{j}"), 1)
                        if j == 0:
                            wait_taken(pe, b, "dtg")
                            wait_room(pe, b, "dtt")
                            for c in range(C):
                                ins = t.transpose(ps("dtt")[:, c * P:(c + 1) * P], dtgT[:, c * P:(c + 1) * P],
                                                  ident[:, :])
                            ins.then_inc(is_full("dtt"), 1)
                        if j == XP:
                            pe.wait_ge(dA_done, b + 1)
                            wait_room(pe, b, "sums")
                            for i, m in enumerate((upto, after, ones)):
                                ins = t.matmul(ps("sums")[:, i * C * NHEADS:(i + 1) * C * NHEADS], m[:, :],
                                               dA[:, :, :].rearrange("p c h -> p (c h)"), start=True, stop=True)
                            ins.then_inc(is_full("sums"), 1)

                    for c in range(C):
                        cols = slice(c * P, (c + 1) * P)
                        if c:
                            wait_taken(pe, b, f"new{c - 1}")
                            wait_room(pe, b, f"off{c}")
                            for q in range(2):
                                ins = t.matmul(ps(f"off{c}")[:, q * 512:(q + 1) * 512], xbc[:, XT + 1, cols],
                                               state[:, q * 512:(q + 1) * 512], start=True, stop=True)
                            ins.then_inc(is_full(f"off{c}"), 1)
                        if c + 1 < C:
                            wait_taken(pe, b, f"cb{c}")
                            pe.wait_ge(xdec_done, b * (C - 1) + c + 1)
                            wait_room(pe, b, f"new{c}")
                            for q in range(2):
                                ins = t.matmul(ps(f"new{c}")[:, q * 512:(q + 1) * 512], btok[:, :],
                                               xdec[:, q * 512:(q + 1) * 512], start=True, stop=True)
                            ins.then_inc(is_full(f"new{c}"), 1)
                        else:
                            turn_next(c)
                        wait_room(pe, b, f"y{c}")
                        wait_taken(pe, b, f"xt{c}")
                        for half in range(2):
                            pe.wait_ge(m_done, b * 2 * C + 2 * c + half + 1)
                            for i in range(HH):
                                h = half * HH + i
                                j, q = divmod(h, P // HD)
                                ins = t.matmul(ps(f"y{c}")[q * HD:(q + 1) * HD, j * P:(j + 1) * P],
                                               xdt[:, h * HD:(h + 1) * HD], decay[:, half, i, :],
                                               start=(j % 4 == 0), stop=(c == 0), skip_group_check=True)
                        if c:
                            wait_taken(pe, b, f"off{c}")
                            for j in range(XT):
                                ins = t.matmul(ps(f"y{c}")[:, j * P:(j + 1) * P],
                                               yoff[:, j * P:(j + 1) * P], ident[:, :],
                                               start=False, stop=True, skip_group_check=True)
                        ins.then_inc(is_full(f"y{c}"), 1)
                        if c + 1 < C:
                            front(c + 1)
                        if c + 1 < C:
                            turn_next(c)

            @block.scalar
            def _(act):
                s = nc.scalar
                with nc.allow_non_contiguous_dma(reason="small parameter tables"):
                    act.wait_ge(const_made, 3)
                    act.dma_start(dtg_raw[:, :, 0:NHEADS], w_cols[:, :, INNER + CONV:]).then_inc(dtg_loaded, 16)
                    for k in range(KH):
                        act.dma_start(dtg_raw[:, k, NHEADS:NHEADS + E],
                                      gate_w[:, k * P:(k + 1) * P].rearrange("e p -> p e")).then_inc(dtg_loaded, 16)
                    act.dma_start(bias_row[:, :], dt_bias.partition_broadcast(P)).then_inc(param_loaded, 16)
                    act.dma_start(cw[:, :, :], conv_w.rearrange("(t p) k -> p t k", p=P)).then_inc(param_loaded, 16)
                    act.dma_start(cb[:, :], conv_b.rearrange("(t p) -> p t", p=P)).then_inc(param_loaded, 16)
                    act.dma_start(a_row[:, :], A.partition_broadcast(P)).then_inc(param_loaded, 16)
                    for i in range(P // HD):
                        act.dma_start(d_col[i * HD:(i + 1) * HD, :],
                                      D.rearrange("(j i) -> i j", i=P // HD)[i].partition_broadcast(HD)
                                      ).then_inc(param_loaded, 16)
                act.wait_ge(dtg_loaded, 16 * (1 + KH))
                s.activation(w_dtg[:, :, :], dtg_raw[:, :, :], ACT.Copy).then_inc(w_hi, 1)
                for k in range(KH):
                    act.wait_ge(xn0_full, k + 1)
                    s.activation(xnT[0][:, k, :], psS[:, k % 2, :], ACT.Copy).then_inc(xnT_hi, 1)
                for n in range(NW):
                    act.wait_ge(w_loaded[n % STAGED], 16 * (n // STAGED + 1))
                    s.activation(w_part[0][:, :, w_slice(n)], w_raw[n % STAGED], ACT.Copy).then_inc(w_hi, 1)

                act.wait_ge(param_loaded, 16 * NPARAM)
                with act.Fori(0, B) as b:
                    def tap(j):
                        wait_full(act, b, f"p{j}")
                        if j >= 2:
                            act.wait_ge(xbc_done, b * XP + j - 1)
                        for i in range(2):
                            ct = 2 * j + i
                            ins = s.activation(acc[:, j % 2, i, :], ps(f"p{j}")[:, i * L:(i + 1) * L],
                                               ACT.Identity, bias=cb[:, ct:ct + 1], scale=cw[:, ct, TAPS - 1:TAPS])
                        ins.then_inc(tap3, 1)

                    def masked(c, half):
                        for i in range(HH):
                            h = half * HH + i
                            ins = s.activation(seg_rhs[1][:, half, i, :], upto[:, :], ACT.Copy,
                                               scale=dA_lo[:, c, h:h + 1])
                        ins.then_inc(seg_lo, 1)

                    def exponents():
                        wait_full(act, b, "sums")
                        s.activation(ex[:, :, :, :].rearrange("p a c h -> p (a c h)"),
                                     ps("sums")[:, 0:3 * C * NHEADS], ACT.Exp).then_inc(is_taken("sums"), 1)

                    def front(c):
                        wait_full(act, b, f"cb{c}")
                        act.wait_ge(cbm_done, b * C + c + 1)
                        if c:
                            wait_full(act, b, f"new{c - 1}")
                        s.activation(btok[:, :], ps(f"cb{c}")[:, P:2 * P], ACT.Copy).then_inc(is_taken(f"cb{c}"), 1)
                        for half in range(2):
                            if c and not half:
                                wait_full(act, b, f"y{c - 1}")
                            wait_full(act, b, f"seg{c}{half}")
                            s.activation(decay[:, half].rearrange("p h l -> p (h l)"), ps(f"seg{c}{half}"),
                                         ACT.Exp).then_inc(is_taken(f"seg{c}{half}"), 1)

                    wait_full(act, b, "dtg")
                    s.activation(dtgT[:, :], ps("dtg"), ACT.Copy).then_inc(is_taken("dtg"), 1)
                    tap(0)
                    act.wait_ge(dt_neg, b + 1)
                    s.activation(u[:, :, :], tmp[:, :, :], ACT.Exp).then_inc(dt_exp, 1)
                    tap(1)
                    act.wait_ge(dt_one, b + 1)
                    s.activation(ln_w[:, :, :], w1[:, :, :], ACT.Ln).then_inc(dt_ln, 1)
                    for j in range(XP):
                        wait_taken(act, b, f"p{j}")
                        s.activation(xbc[:, 2 * j:2 * j + 2, :], acc[:, j % 2, :, :], ACT.Silu
                                     ).then_inc(xbc_done, 1)
                        if j + 2 < XP:
                            tap(j + 2)
                        if j in (XP - 3, XP - 2):
                            act.wait_ge(dA_done, b + 1)
                            masked(0, j - (XP - 3))
                    for j in range(XP, PAIRS):
                        if j == FRONT_AT:
                            exponents()
                            front(0)
                            for half in range(2):
                                masked(1, half)
                        if j == XP:
                            act.wait_ge(rows_zeroed, 32)
                        wait_full(act, b, f"p{j}")
                        i = 2 * (j - XP)
                        s.activation(zs[:, i:i + 2, :].rearrange("p t l -> p (t l)"), ps(f"p{j}"), ACT.Silu
                                     ).then_inc(is_taken(f"p{j}"), 1)
                    for c in range(C):
                        if c + 1 < C:
                            front(c + 1)
                        wait_full(act, b, f"xn{c}")
                        s.activation(xnT[0][:, c, :], ps(f"xn{c}"), ACT.Copy).then_inc(xnT_hi, 1)
                        if c + 2 < C:
                            for half in range(2):
                                masked(c + 2, half)

            @block.vector
            def _(dve):
                v = nc.vector
                for n, slot in enumerate(taken["S"] + taken["D"]):
                    v.memset(nothing[:, n:n + 1], 0.0).then_inc(slot, 1)
                for i in range(2):
                    v.memset(nothing[:, 5 + i:6 + i], 0.0).then_inc(y_stored[i], 16)

                n_own = [0, 0]

                def then_read(ins):
                    n_own[0] += 1
                    ins.then_inc(own, 1)
                    dve.wait_ge(own, n_own[1] + n_own[0])

                def layernorm(n):
                    dve.wait_ge(x_loaded, n * 16)
                    for c in range(C):
                        ins = v.bn_stats(stats[:, c, :], xrow[:, c, :])
                    then_read(ins)
                    v.memset(nothing[:, 7:8], 0.0)
                    for c in range(C):
                        ins = v.bn_aggr(mv[:, c, :], stats[:, c, :])
                    then_read(ins)
                    then_read(v.tensor_scalar(nwt[:, 0, :], mv[:, :, 1], 1e-5, None, ALU.add))
                    then_read(v.tensor_scalar(rstd[:, :].bitcast(I32), nwt[:, 0, :].bitcast(I32),
                                              -0.5, 1597463007.0, ALU.mult, ALU.add))
                    for _ in range(4):
                        then_read(v.tensor_tensor(nwt[:, 1, :], rstd[:, :], rstd[:, :], ALU.mult))
                        then_read(v.scalar_tensor_tensor(out=nwt[:, 2, :], in0=nwt[:, 1, :], scalar=-0.5,
                                                         in1=nwt[:, 0, :], op0=ALU.mult, op1=ALU.mult))
                        then_read(v.scalar_tensor_tensor(out=rstd[:, :], in0=nwt[:, 2, :], scalar=1.5,
                                                         in1=rstd[:, :], op0=ALU.add, op1=ALU.mult))
                    for c in range(C):
                        ins = v.tensor_scalar(xrow[:, c, :], xrow[:, c, :], mv[:, c, 0:1], rstd[:, c:c + 1],
                                              ALU.subtract, ALU.mult)
                    ins.then_inc(ln_done, 1)

                layernorm(1)
                for k in range(KH):
                    dve.wait_ge(xnT_hi, k + 1)
                    v.tensor_tensor(xnT[1][:, k, :], psS[:, k % 2, :], xnT[0][:, k, :].bitcast(F32),
                                    ALU.subtract).then_inc(xnT_lo, 1)
                dve.wait_ge(w_hi, 1)
                v.tensor_tensor(w_dtg[:, :, DL:2 * DL], dtg_raw[:, :, 0:DL], w_dtg[:, :, 0:DL].bitcast(F32),
                                ALU.subtract).then_inc(w_lo, 1)
                dve.wait_ge(const_made, 6)
                v.tensor_copy(after_r[:, :], after[:, :]).then_inc(w_lo, 1)
                for n in range(NW):
                    dve.wait_ge(w_hi, n + 2)
                    cols = w_slice(n)
                    v.tensor_tensor(w_part[1][:, :, cols], w_raw[n % STAGED], w_part[0][:, :, cols].bitcast(F32),
                                    ALU.subtract).then_inc(w_lo, 1)
                dve.wait_ge(param_loaded, 16 * NPARAM)
                before_loop = n_own[0]

                with dve.Fori(0, B) as b:
                    n_own[:] = [before_loop, b * OWN]

                    def conv_pair(j):
                        dve.wait_ge(tap3, b * XP + j + 1)
                        for tap in range(TAPS - 2, -1, -1):
                            sh = TAPS - 1 - tap
                            for i in range(2):
                                ct = 2 * j + i
                                a = acc[:, j % 2, i, sh:L]
                                ins = v.scalar_tensor_tensor(out=a, in0=ps(f"p{j}")[:, i * L:(i + 1) * L - sh],
                                                             scalar=cw[:, ct, tap:tap + 1], in1=a,
                                                             op0=ALU.mult, op1=ALU.add)
                            if tap:
                                then_read(ins)
                        ins.then_inc(is_taken(f"p{j}"), 1)

                    def turned(c):
                        dve.wait_ge(xnT_hi, b * KH + KH + c + 1)
                        v.tensor_tensor(xnT[1][:, c, :], ps(f"xn{c}"), xnT[0][:, c, :].bitcast(F32),
                                        ALU.subtract).then_inc(xnT_lo, 1)
                        dve.wait_ge(xnT_lo, b * KH + KH + c + 1)
                        v.memset(nothing[:, 7:8], 0.0).then_inc(is_taken(f"xn{c}"), 1)

                    wait_full(dve, b, "dtt")
                    got = ps("dtt").rearrange("p (c n) -> p c n", n=P)
                    v.tensor_copy(logits_b[:, :, :], got[:, :, NHEADS:NHEADS + E])
                    then_read(v.tensor_tensor(dt_in[:, :, :], got[:, :, 0:NHEADS],
                                              bias_row[:, :].unsqueeze(1).to_broadcast([P, C, NHEADS]), ALU.add))
                    v.tensor_tensor(logits_b[:, :, :], logits_b[:, :, :], got[:, :, DL + NHEADS:DL + NHEADS + E],
                                    ALU.add)
                    v.tensor_tensor(dt_in[:, :, :], dt_in[:, :, :], got[:, :, DL:DL + NHEADS], ALU.add
                                    ).then_inc(is_taken("dtt"), 1)
                    wait_taken(dve, b, "dtt")
                    v.scalar_tensor_tensor(out=tmp[:, :, :], in0=dt_in[:, :, :], scalar=-1.0, in1=dt_in[:, :, :],
                                           op0=ALU.mult, op1=ALU.min).then_inc(dt_neg, 1)
                    conv_pair(0)
                    dve.wait_ge(dt_exp, b + 1)
                    v.tensor_scalar(w1[:, :, :], u[:, :, :], 1.0, None, ALU.add).then_inc(dt_one, 1)
                    conv_pair(1)
                    v.reciprocal(dA[:, :, :], w1[:, :, :])
                    then_read(v.tensor_scalar(tmp[:, :, :], w1[:, :, :], -1.0, None, ALU.add))
                    then_read(v.tensor_tensor(tmp[:, :, :], u[:, :, :], tmp[:, :, :], ALU.subtract))
                    then_read(v.tensor_tensor(tmp[:, :, :], tmp[:, :, :], dA[:, :, :], ALU.mult))
                    dve.wait_ge(dt_ln, b + 1)
                    then_read(v.tensor_tensor(tmp[:, :, :], tmp[:, :, :], ln_w[:, :, :], ALU.add))
                    then_read(v.scalar_tensor_tensor(out=dt_[:, :, :], in0=dt_in[:, :, :], scalar=0.0,
                                                     in1=tmp[:, :, :], op0=ALU.max, op1=ALU.add))
                    then_read(v.tensor_tensor(dA[:, :, :], dt_[:, :, :],
                                              a_row[:, :].unsqueeze(1).to_broadcast([P, C, NHEADS]), ALU.mult))
                    then_read(v.tensor_copy(dA_hi[:, :, :], dA[:, :, :]))
                    v.tensor_tensor(dA_lo[:, :, :], dA[:, :, :], dA_hi[:, :, :].bitcast(F32), ALU.subtract
                                    ).then_inc(dA_done, 1)
                    for j in range(2, XP):
                        conv_pair(j)

                    def state_part(c):
                        wait_full(dve, b, f"off{c}")
                        if c == 1:
                            wait_taken(dve, b, "sums")
                        v.tensor_tensor(heads(yoff[:, :]), heads(ps(f"off{c}")), by_head(ex[:, 0, c]), ALU.mult
                                        ).then_inc(is_taken(f"off{c}"), 1)

                    def gate_y(c):
                        wait_taken(dve, b, f"y{c}")
                        y = ybuf[:, c % 2]
                        v.tensor_tensor(y, y, zs[:, :, c * P:(c + 1) * P], ALU.mult).then_inc(y_done, 1)

                    def front(c):
                        wait_full(dve, b, f"cb{c}")
                        v.tensor_tensor(cbm[:, :], ps(f"cb{c}")[:, 0:P], upto[:, :], ALU.mult).then_inc(cbm_done, 1)
                        wait_full(dve, b, f"xt{c}")
                        if c:
                            wait_full(dve, b, f"y{c - 1}")
                            dve.wait_ge(xdec_done, b * (C - 1) + c)
                        v.tensor_tensor(heads(xdt[:, :]), heads(ps(f"xt{c}")), by_head(dt_[:, c]), ALU.mult
                                        ).then_inc(is_taken(f"xt{c}"), 1)
                        for half in range(2):
                            wait_taken(dve, b, f"seg{c}{half}")
                            if not half:
                                dve.wait_ge(cbm_done, b * C + c + 1)
                            v.tensor_tensor(decay[:, half], decay[:, half],
                                            cbm[:, :].unsqueeze(1).to_broadcast([P, HH, P]), ALU.mult
                                            ).then_inc(m_done, 1)
                        if c:
                            state_part(c)

                    front(0)
                    layernorm(b + 2)
                    v.tensor_copy(logits[:, bass.ds(b * C, C), :], logits_b[:, :, :])
                    for c in range(C):
                        ins = v.max(best_b[:, c, :], logits_b[:, c, :])
                    then_read(ins)
                    v.memset(nothing[:, 7:8], 0.0)
                    for c in range(C):
                        ins = v.max_index(best_at_b[:, c, :], best_b[:, c, :], logits_b[:, c, :])
                    then_read(ins)
                    v.tensor_copy(choice[:, :, bass.ds(b * C, C)], best_at_b[:, :, 0:2].rearrange("p t k -> p k t"))
                    v.tensor_copy(top[:, bass.ds(b * C, C)], best_b[:, :, 0])
                    for c in range(C):
                        if c + 1 < C:
                            if c:
                                dve.wait_ge(state_scaled, b * (C - 2) + c)
                            wait_full(dve, b, f"new{c}")
                            if c:
                                ins = v.tensor_tensor(state[:, :], ps(f"new{c}"), state[:, :], ALU.add)
                            else:
                                ins = v.tensor_copy(state[:, :], ps(f"new{c}"))
                            ins.then_inc(is_taken(f"new{c}"), 1)
                        if c:
                            gate_y(c - 1)
                            turned(c - 1)
                        if c + 1 == C:
                            turned(c)
                        wait_full(dve, b, f"y{c}")
                        dve.wait_ge(y_stored[c % 2], (b * (C // 2) + c // 2 + 1) * 16)
                        dve.wait_ge(xD_done, b * C + c + 1)
                        v.tensor_tensor(ybuf[:, c % 2], ps(f"y{c}").rearrange("p (j l) -> p j l", l=P), xD[:, :, :],
                                        ALU.add).then_inc(is_taken(f"y{c}"), 1)
                        if c + 1 < C:
                            front(c + 1)
                    gate_y(C - 1)
                    assert n_own[0] - before_loop == OWN, n_own[0] - before_loop

        weight = [keep(f"weight_{k}", [P, NT]) for k in range(TOP)]
        row_of = [keep(f"row_of_{k}", [P, NT], U32) for k in range(TOP)]
        token_of = keep("token_of", [P, NQ], U32)
        first_pair = keep("first_pair", [P, E + 1], I32)

        KI = -(-I // P)
        GU = KH * 2 * I
        WS = GU + KI * H
        FULL_COLS = GU + (I // P) * H
        REST = I - (I // P) * P
        DVE_COLS = FULL_COLS // 2 // 16 * 16
        WE_PIECES = ((slice(0, P), slice(0, FULL_COLS)), (slice(0, REST), slice(FULL_COLS, WS)))
        WE_SHARES = (((slice(0, P), slice(0, DVE_COLS)),), ((slice(0, P), slice(DVE_COLS, FULL_COLS)), WE_PIECES[1]))
        assert PAIR <= 256
        SF = IS // P
        NJ = SF + 1
        HALF = P // 2
        SK = 2 * IS
        SGU = KH * SK
        SKA = KH - 1
        assert IS == SF * P + HALF
        ws = [keep(f"ws_{p}", [P, SGU + NJ * H], F32R) for p in ("hi", "lo")]

        def sw_cols(k, j, g):
            if j < SF and g:
                return slice(k * SK + SF * P + P + j * P, k * SK + SF * P + P + (j + 1) * P)
            return slice(k * SK + j * P, k * SK + (j + 1) * P)

        def h_part(j):
            return slice(0, P) if j < SF else slice(HALF, P)

        xnrow_c = keep("c_xnrow", [P, C, H])
        experts_weights = outer.enter_context(ExitStack())
        we = [[experts_weights.enter_context(nc.sbuf_tensor(f"we_{p}{i}", [P, WS], F32R)) for p in ("hi", "lo")]
              for i in range(2)]
        B_COLS = SGU + NJ * H - SKA * SK
        we_raw = experts_weights.enter_context(nc.sbuf_tensor("we_raw", [P, max(WS, B_COLS)], F32))

        def k_rows(j):
            return min(P, I - j * P)

        def load_expert(e, dst, n, loaded):
            gu = dst[:, 0:GU].rearrange("p (k g i) -> p k g i", k=KH, g=2)
            e.dma_start(gu[:, :, 0, :], w_gate[n].rearrange("(k p) i -> p k i", p=P)).then_inc(loaded, 16)
            e.dma_start(gu[:, :, 1, :], w_up[n].rearrange("(k p) i -> p k i", p=P)).then_inc(loaded, 16)
            full = I // P
            e.dma_start(dst[:, GU:FULL_COLS].rearrange("p (k n) -> p k n", k=full),
                        w_down[n, 0:full * P, :].rearrange("(k p) n -> p k n", p=P)).then_inc(loaded, 16)
            e.dma_start(dst[0:REST, FULL_COLS:WS], w_down[n, full * P:I, :]).then_inc(loaded, 16)

        def load_shared(e, dst, k0, k1, loaded):
            to = dst[:, 0:(k1 - k0) * SK].rearrange("p (k c) -> p k c", c=SK)
            g, u = (w[k0 * P:k1 * P, :].rearrange("(k p) c -> p k c", p=P) for w in (sw_gate, sw_up))
            e.dma_start(to[:, :, 0:IS], g).then_inc(loaded, 16)
            e.dma_start(to[:, :, IS:IS + HALF], u[:, :, SF * P:]).then_inc(loaded, 16)
            e.dma_start(to[:, :, IS + HALF:], u[:, :, 0:SF * P]).then_inc(loaded, 16)

        stage = ExitStack()
        with stage:
            def sb(name, shape, dt=F32):
                return stage.enter_context(nc.sbuf_tensor(name, shape, dt))

            def sem(name):
                return stage.enter_context(nc.semaphore(name))

            GROUP = 8
            NG = TOP * NT // GROUP
            iota_e = sb("iota_e", [P, E])
            iota_q = sb("iota_q", [P, P])
            token_id = sb("token_id", [P, NT])
            picked = [sb(f"picked_{k}", [P, E, NT]) for k in range(TOP)]
            either = sb("either", [P, E, NT])
            shifted = sb("shifted", [P, NT, E])
            total = sb("total", [P, NT])
            one_row = sb("one_row", [P, E * NT])
            tile_sum = sb("tile_sum", [P, E, NT])
            before = sb("before", [P, E, NT])
            upto_sum = sb("upto_sum", [P, E, NT])
            pairs = sb("pairs", [P, E])
            pair_end = sb("pair_end", [P, E + 1])
            base = sb("base", [P, E, NT])
            rows = sb("rows", [P, TOP, NT])
            tile_q = sb("tile_q", [P, TOP, NT])
            tile_r = sb("tile_r", [P, TOP, NT])
            hot_r = sb("hot_r", [P, 2, GROUP, P], F32R)
            hot_q = sb("hot_q", [P, 2, GROUP, NQ], F32R)
            psR = stage.enter_context(nc.psum_tensor("psR", [P, 3, 512], F32))

            iotas = sem("iotas")
            own = sem("r_own")
            picks = sem("picks")
            shifted_done = sem("shifted_done")
            exp_done = sem("r_exp")
            counted = sem("counted")
            hot = sem("hot")
            placed = sem("placed")
            w_in = [sem(f"r_w{n}_loaded") for n in range(3)]
            w_hi = sem("r_w_hi")
            w_lo = sem("r_w_lo")
            A_COLS = SKA * SK
            B_FULL = SGU + SF * H - A_COLS
            B_DVE = B_FULL * 3 // 5 // 16 * 16
            EARLY = 2
            B_EARLY = (KH - SKA) * SK + EARLY * H
            w_raw = [we_raw, sb("r_w_raw", [P, A_COLS])]
            every = slice(0, P)
            w_sets = (
                (w_raw[0], we[0][0][:, :], we[0][1][:, :], 4,
                 ((every, slice(0, B_EARLY)), (every, slice(B_EARLY, FULL_COLS)), WE_PIECES[1]), ()),
                (w_raw[1], ws[0][:, 0:A_COLS], ws[1][:, 0:A_COLS], 3, ((every, slice(0, A_COLS)),), ()),
                (w_raw[0], ws[0][:, A_COLS:], ws[1][:, A_COLS:], 6,
                 ((every, slice(B_DVE, B_FULL)),),
                 ((every, slice(0, B_DVE)), (slice(HALF, P), slice(B_FULL, B_FULL + H)))),
            )
            ROUND = 12582912.0
            block = stage.enter_context(nc.Block())

            @block.gpsimd
            def _(pool):
                g = nc.gpsimd
                g.iota(iota_e[:, :], pattern=[[1, E]], base=0, channel_multiplier=0,
                       allow_small_or_imprecise_dtypes=True).then_inc(iotas, 1)
                g.iota(iota_q[:, :], pattern=[[1, P]], base=0, channel_multiplier=0,
                       allow_small_or_imprecise_dtypes=True).then_inc(iotas, 1)
                g.iota(token_id[:, :], pattern=[[P, NT]], base=0, channel_multiplier=1,
                       allow_small_or_imprecise_dtypes=True).then_inc(iotas, 1)
                for n, (raw, hi, lo, _, by_pool, _) in enumerate(w_sets):
                    pool.wait_ge(w_hi, n + 1)
                    for i, (part, cols) in enumerate(by_pool):
                        ins = g.tensor_tensor(lo[part, cols], raw[part, cols], hi[part, cols].bitcast(F32),
                                              ALU.subtract)
                        if n == 0 and i == 0:
                            ins.then_inc(w_lo, 1)
                    ins.then_inc(w_lo, 1)
                pool.wait_ge(w_lo, len(w_sets) + 1)

            @block.sync
            def _(sp):
                load_expert(sp, w_raw[0], 0, w_in[0])
                for i in range(2):
                    sp.wait_ge(y_stored[i], 16 + 16 * B * C // 2)
                load_shared(sp, w_raw[1], 0, SKA, w_in[1])
                sp.wait_ge(w_lo, 1)
                load_shared(sp, w_raw[0], SKA, KH, w_in[2])
                down = w_raw[0][:, (KH - SKA) * SK:(KH - SKA) * SK + NJ * H].rearrange("p (j n) -> p j n", n=H)
                rows = sw_down[0:SF * P, :].rearrange("(j p) n -> p j n", p=P)
                sp.dma_start(down[:, 0:EARLY, :], rows[:, 0:EARLY, :]).then_inc(w_in[2], 16)
                sp.wait_ge(w_lo, 2)
                sp.dma_start(down[:, EARLY:SF, :], rows[:, EARLY:, :]).then_inc(w_in[2], 16)
                sp.dma_start(down[HALF:P, SF, :], sw_down[SF * P:, :]).then_inc(w_in[2], 16)

            @block.scalar
            def _(act):
                s = nc.scalar
                act.wait_ge(shifted_done, 1)
                s.activation(shifted[:, :, :], shifted[:, :, :], ACT.Exp).then_inc(exp_done, 1)
                for n, (raw, hi, _, transfers, by_pool, by_dve) in enumerate(w_sets):
                    act.wait_ge(w_in[n], 16 * transfers)
                    for part, cols in (*by_dve, *by_pool):
                        ins = s.activation(hi[part, cols], raw[part, cols], ACT.Copy)
                    ins.then_inc(w_hi, 1)

            @block.tensor
            def _(pe):
                t = nc.tensor
                pe.wait_ge(picks, 1)
                flat = either[:, :, :].rearrange("p e t -> p (e t)")
                t.matmul(psR[:, 0, 0:E * NT], upto[:, :], flat, start=True, stop=True)
                t.matmul(psR[:, 1, 0:E * NT], ones[:, :], flat, start=True, stop=True).then_inc(counted, 1)
                for n in range(NG):
                    pe.wait_ge(hot, n + 1)
                    for i in range(GROUP):
                        ins = t.matmul(psR[:, 2, 0:NQ], hot_r[:, n % 2, i, :], hot_q[:, n % 2, i, :],
                                       start=(n == 0 and i == 0), stop=(n == NG - 1 and i == GROUP - 1))
                    ins.then_inc(placed, 1)

            @block.vector
            def _(dve):
                v = nc.vector
                n_own = [0]

                def then_read(ins):
                    n_own[0] += 1
                    ins.then_inc(own, 1)
                    dve.wait_ge(own, n_own[0])

                v.tensor_tensor(shifted[:, :, :], logits[:, :, :], top[:, :].unsqueeze(2).to_broadcast([P, NT, E]),
                                ALU.subtract).then_inc(shifted_done, 1)
                v.memset(one_row[:, :], 1.0)
                dve.wait_ge(iotas, 3)
                for k in range(TOP):
                    ins = v.tensor_tensor(picked[k][:, :, :], iota_e[:, :].unsqueeze(2).to_broadcast([P, E, NT]),
                                          choice[:, k].unsqueeze(1).to_broadcast([P, E, NT]), ALU.is_equal)
                then_read(ins)
                v.tensor_tensor(either[:, :, :], picked[0][:, :, :], picked[1][:, :, :], ALU.add).then_inc(picks, 1)
                dve.wait_ge(exp_done, 1)
                then_read(v.tensor_reduce(total[:, :], shifted[:, :, :], AX.X, ALU.add))
                then_read(v.reciprocal(weight[0][:, :], total[:, :]))
                then_read(v.tensor_tensor(base[:, :, :], picked[1][:, :, :],
                                          shifted[:, :, :].rearrange("p t e -> p e t"), ALU.mult))
                then_read(v.tensor_reduce(weight[1][:, :], base[:, :, :].rearrange("p e t -> p t e"), AX.X, ALU.add))
                then_read(v.tensor_tensor(weight[1][:, :], weight[1][:, :], weight[0][:, :], ALU.mult))
                dve.wait_ge(counted, 1)
                flat = [x[:, :, :].rearrange("p e t -> p (e t)") for x in (tile_sum, upto_sum, before)]
                then_read(v.tensor_copy(flat[0], psR[:, 1, 0:E * NT]))
                then_read(v.tensor_tensor_scan(flat[1], one_row[:, :], flat[0], 0.0, ALU.mult, ALU.add))
                then_read(v.tensor_tensor(flat[2], flat[1], flat[0], ALU.subtract))
                then_read(v.tensor_tensor(pairs[:, :], upto_sum[:, :, NT - 1], before[:, :, 0], ALU.subtract))
                then_read(v.tensor_scalar(pairs[:, :], pairs[:, :], 1.0 / PAIR, 0.5 - 0.5 / PAIR, ALU.mult, ALU.add))
                then_read(v.tensor_scalar(pairs[:, :], pairs[:, :], ROUND, None, ALU.add))
                then_read(v.tensor_scalar(pairs[:, :], pairs[:, :], -ROUND, 1.0, ALU.add, ALU.max))
                v.memset(pair_end[:, 0:1], 0.0)
                then_read(v.tensor_tensor_scan(pair_end[:, 1:E + 1], one_row[:, 0:E], pairs[:, :], 0.0,
                                               ALU.mult, ALU.add))
                v.tensor_copy(first_pair[:, :], pair_end[:, :])
                then_read(v.scalar_tensor_tensor(out=pairs[:, :], in0=pair_end[:, 0:E], scalar=float(PAIR),
                                                 in1=before[:, :, 0], op0=ALU.mult, op1=ALU.subtract))
                then_read(v.tensor_tensor(base[:, :, :], before[:, :, :], psR[:, 0, 0:E * NT]
                                          .rearrange("p (e t) -> p e t", t=NT), ALU.add))
                then_read(v.scalar_tensor_tensor(out=base[:, :, :], in0=base[:, :, :], scalar=-1.0,
                                                 in1=pairs[:, :].unsqueeze(2).to_broadcast([P, E, NT]),
                                                 op0=ALU.add, op1=ALU.add))
                for k in range(TOP):
                    ins = v.tensor_tensor(picked[k][:, :, :], picked[k][:, :, :], base[:, :, :], ALU.mult)
                then_read(ins)
                for k in range(TOP):
                    ins = v.tensor_reduce(rows[:, k], picked[k][:, :, :].rearrange("p e t -> p t e"), AX.X, ALU.add)
                then_read(ins)
                for k in range(TOP):
                    v.tensor_copy(row_of[k][:, :], rows[:, k])
                then_read(v.tensor_scalar(tile_q[:, :, :], rows[:, :, :], 1.0 / P, 0.5 / P - 0.5, ALU.mult, ALU.add))
                then_read(v.tensor_scalar(tile_q[:, :, :], tile_q[:, :, :], ROUND, None, ALU.add))
                then_read(v.tensor_scalar(tile_q[:, :, :], tile_q[:, :, :], -ROUND, None, ALU.add))
                then_read(v.scalar_tensor_tensor(out=tile_r[:, :, :], in0=tile_q[:, :, :], scalar=-float(P),
                                                 in1=rows[:, :, :], op0=ALU.mult, op1=ALU.add))
                for n in range(NG):
                    if n >= 2:
                        dve.wait_ge(placed, n - 1)
                    k, t = divmod(n * GROUP, NT)
                    ts = slice(t, t + GROUP)
                    v.tensor_tensor(hot_q[:, n % 2], iota_q[:, 0:NQ].unsqueeze(1).to_broadcast([P, GROUP, NQ]),
                                    tile_q[:, k, ts].unsqueeze(2).to_broadcast([P, GROUP, NQ]), ALU.is_equal
                                    ).then_inc(own, 1)
                    n_own[0] += 1
                    v.tensor_tensor(hot_r[:, n % 2], iota_q[:, :].unsqueeze(1).to_broadcast([P, GROUP, P]),
                                    tile_r[:, k, ts].unsqueeze(2).to_broadcast([P, GROUP, P]), ALU.is_equal)
                    dve.wait_ge(own, n_own[0])
                    v.tensor_tensor(hot_q[:, n % 2], hot_q[:, n % 2].bitcast(F32),
                                    token_id[:, ts].unsqueeze(2).to_broadcast([P, GROUP, NQ]), ALU.mult
                                    ).then_inc(hot, 1)
                dve.wait_ge(w_hi, len(w_sets))
                raw, hi, lo, _, _, by_dve = w_sets[-1]
                for part, cols in by_dve:
                    v.tensor_tensor(lo[part, cols], raw[part, cols], hi[part, cols].bitcast(F32), ALU.subtract)
                dve.wait_ge(placed, NG)
                v.tensor_copy(token_of[:, :], psR[:, 2, 0:NQ])

        stage = ExitStack()
        with stage:
            def sb(name, shape, dt=F32):
                return stage.enter_context(nc.sbuf_tensor(name, shape, dt))

            def sem(name):
                return stage.enter_context(nc.semaphore(name))

            which = [sb(f"which{h}", [P, 1], U32) for h in range(HALVES)]
            tick = sb("tick", [P, 1])
            nothing = sb("b_nothing", [P, 16])
            xs = sb("xs", [P, HALVES, H])
            xsT = [sb(f"xsT_{p}", [P, KH, PAIR], F32R) for p in ("hi", "lo")]
            gate = sb("gate", [P, KI, PAIR])
            hid = sb("hid", [P, KI, PAIR])
            hidT = [sb(f"hidT_{p}", [P, KI, PAIR], F32R) for p in ("hi", "lo")]
            eo = sb("eo", [P, HALVES, H])
            psT = stage.enter_context(nc.psum_tensor("psT", [P, HALVES, 512], F32))
            psG = stage.enter_context(nc.psum_tensor("psG", [P, KI, 2, 256], F32))
            psO = stage.enter_context(nc.psum_tensor("psO", [P, HALVES, 512], F32))

            xn0_loaded = sem("b_xn0_loaded")
            we_loaded = sem("we_loaded")
            we_hi = sem("we_hi")
            we_lo = sem("we_lo")
            we_lo_pool = sem("we_lo_pool")
            tick_made = sem("tick_made")
            which_done = sem("which_done")
            xs_loaded = [sem(f"xs{h}_loaded") for h in range(HALVES)]
            xsT_full = sem("xsT_full")
            xsT_hi = sem("xsT_hi")
            xsT_lo = sem("xsT_lo")
            gu_full = sem("gu_full")
            gate_done = sem("gate_done")
            hid_done = sem("hid_done")
            hid_hi = sem("hid_hi")
            hid_lo = sem("hid_lo")
            eo_full = sem("eo_full")
            eo_done = sem("eo_done")
            eo_stored = [sem(f"eo{h}_stored") for h in range(HALVES)]
            block = stage.enter_context(nc.Block())

            def start_of(e, i):
                return e.value_load(first_pair[0:1, bass.ds(i, 1)], min_val=0, max_val=MAX_PAIRS)

            def experts(e, each, tile_pair):
                with e.Fori(0, E // 2) as two:
                    for slot in range(2):
                        expert = two * 2 + slot
                        first, end = start_of(e, expert), start_of(e, expert + 1)
                        each(expert, slot)
                        with e.Fori(first, end) as pair:
                            tile_pair(pair, slot)

            @block.sync
            def _(sp):
                load_expert(sp, we_raw, 1, we_loaded)
                sp.dma_start(xnrow_c[:, :, :], xn_tok[0]).then_inc(xn0_loaded, 16)

                def each(expert, slot):
                    sp.wait_ge(we_lo, expert + 2)
                    sp.wait_ge(we_lo_pool, expert + 2)
                    load_expert(sp, we_raw, (expert + 2) % E, we_loaded)

                def tile_pair(pair, slot):
                    for h in range(HALVES):
                        sp.wait_ge(eo_done, pair * HALVES + h + 3)
                        sp.dma_start(eo_rows[pair * HALVES + h], eo[:, h, :]).then_inc(eo_stored[h], 16)

                experts(sp, each, tile_pair)
                sp.wait_ge(we_loaded, 64 * (E + 1))
                sp.wait_ge(xn0_loaded, 16)

            @block.gpsimd
            def _(pool):
                g = nc.gpsimd
                g.memset(tick[:, :], 0.0).then_inc(tick_made, 1)
                pool.wait_ge(tick_made, 1)
                g.memset(tick[:, :], 0.0).then_inc(we_lo_pool, 1)
                pool.wait_ge(we_lo_pool, 1)

                def fetch(pair):
                    for h in range(HALVES):
                        n = pair * HALVES + h
                        pool.wait_ge(xsT_full, n + 1)
                        g.tensor_copy(which[h][:, :], token_of[:, bass.ds(n, 1)]).then_inc(which_done, 1)
                        pool.wait_ge(which_done, n + 1)
                        g.tensor_tensor(tick[:, :], tick[:, :], tick[:, :], ALU.add)
                        g.indirect_dma_start(out=xs[:, h, :], out_offset=None, in_=xn_dram[:, :],
                                             in_offset=bass.IndirectOffsetOnAxis(ap=which[h][:, 0:1], axis=0)
                                             ).then_inc(xs_loaded[h], 16)

                def split(expert, slot):
                    pool.wait_ge(we_hi, expert * 2 + 2)
                    for rows, cols in WE_SHARES[1]:
                        ins = g.tensor_tensor(we[1 - slot][1][rows, cols], we_raw[rows, cols],
                                              we[1 - slot][0][rows, cols].bitcast(F32), ALU.subtract)
                    ins.then_inc(we_lo_pool, 1)

                for pair in range(FETCH_AHEAD):
                    fetch(pair)
                experts(pool, split, lambda pair, slot: fetch(pair + FETCH_AHEAD))
                n_pairs = start_of(pool, E)
                for h in range(HALVES):
                    pool.wait_ge(eo_stored[h], n_pairs * 16 + 16)
                    pool.wait_ge(xs_loaded[h], n_pairs * 16 + 16 * FETCH_AHEAD)

            @block.tensor
            def _(pe):
                t = nc.tensor

                def turn(pair, h):
                    pe.wait_ge(xs_loaded[h], pair * 16 + 16)
                    pe.wait_ge(xsT_lo, pair * HALVES + h + 1)
                    for k in range(KH):
                        ins = t.transpose(psT[:, h, k * P:(k + 1) * P], xs[:, h, k * P:(k + 1) * P], ident[:, :])
                    ins.then_inc(xsT_full, 1)

                def gate_up(pair, slot, j):
                    rows = k_rows(j)
                    pe.wait_ge(hid_done, pair * KI + j + 1)
                    for g in range(2):
                        m = 0
                        for k in range(KH):
                            c0 = (2 * k + g) * I + j * P
                            for a, c in PARTS:
                                ins = t.matmul(psG[0:rows, j, g, 0:PAIR], we[slot][a][:, c0:c0 + rows],
                                               xsT[c][:, k, :], start=(m == 0), stop=(m == 3 * KH - 1))
                                m += 1
                    ins.then_inc(gu_full, 1)

                def down(pair, slot, h):
                    pe.wait_ge(eo_done, pair * HALVES + h + 1)
                    m = 0
                    for k in range(KI):
                        rows = k_rows(k)
                        if h == 0:
                            pe.wait_ge(hid_lo, pair * KI + k + 1 + KI)
                        for a, c in PARTS:
                            ins = t.matmul(psO[:, h, :], hidT[a][0:rows, k, h * P:(h + 1) * P],
                                           we[slot][c][0:rows, GU + k * H:GU + (k + 1) * H],
                                           start=(m == 0), stop=(m == 3 * KI - 1))
                            m += 1
                    ins.then_inc(eo_full, 1)

                def tile_pair(pair, slot):
                    pe.wait_ge(xsT_lo, pair * HALVES + 4)
                    for j in range(KI):
                        gate_up(pair, slot, j)
                    for h in range(HALVES):
                        turn(pair + 1, h)
                    for h in range(HALVES):
                        down(pair, slot, h)

                for h in range(HALVES):
                    turn(0, h)

                def each(expert, slot):
                    pe.wait_ge(const_made, 6)
                    pe.wait_ge(we_lo, expert + 1)
                    pe.wait_ge(we_lo_pool, expert + 1)

                experts(pe, each, tile_pair)

            @block.scalar
            def _(act):
                s = nc.scalar

                def split(expert, slot):
                    act.wait_ge(we_loaded, expert * 64 + 64)
                    for share in WE_SHARES:
                        for rows, cols in share:
                            ins = s.activation(we[1 - slot][0][rows, cols], we_raw[rows, cols], ACT.Copy)
                        ins.then_inc(we_hi, 1)

                def turned(pair, h):
                    act.wait_ge(xsT_full, pair * HALVES + h + 3)
                    s.activation(xsT[0][:, :, h * P:(h + 1) * P], psT[:, h, :].rearrange("p (k n) -> p k n", n=P),
                                 ACT.Copy).then_inc(xsT_hi, 1)

                def silu(pair, j):
                    rows = k_rows(j)
                    act.wait_ge(gu_full, pair * KI + j + 1)
                    s.activation(gate[0:rows, j, :], psG[0:rows, j, 0, 0:PAIR], ACT.Silu).then_inc(gate_done, 1)

                def hidden(pair, j):
                    rows = k_rows(j)
                    act.wait_ge(hid_done, pair * KI + j + 1 + KI)
                    s.activation(hidT[0][0:rows, j, :], hid[0:rows, j, :], ACT.Copy).then_inc(hid_hi, 1)

                def output(pair, h):
                    act.wait_ge(eo_full, pair * HALVES + h + 1)
                    act.wait_ge(eo_stored[h], pair * 16 + 16)
                    s.activation(eo[:, h, :], psO[:, h, :], ACT.Copy).then_inc(eo_done, 1)

                def tile_pair(pair, slot):
                    silu(pair, 0)
                    for j in range(1, KI):
                        silu(pair, j)
                        hidden(pair, j - 1)
                    hidden(pair, KI - 1)
                    for h in range(HALVES):
                        turned(pair + 1, h)
                    for h in range(HALVES):
                        output(pair, h)

                for h in range(HALVES):
                    turned(0, h)
                experts(act, split, tile_pair)

            @block.vector
            def _(dve):
                v = nc.vector
                for n, (sm, by) in enumerate(((xsT_full, 2), (xsT_lo, 2), (hid_done, KI), (hid_lo, KI), (eo_done, 2),
                                              (eo_stored[0], 16), (eo_stored[1], 16), (we_lo, 1))):
                    v.memset(nothing[:, n:n + 1], 0.0).then_inc(sm, by)

                def split(expert, slot):
                    dve.wait_ge(we_hi, expert * 2 + 1)
                    for rows, cols in WE_SHARES[0]:
                        ins = v.tensor_tensor(we[1 - slot][1][rows, cols], we_raw[rows, cols],
                                              we[1 - slot][0][rows, cols].bitcast(F32), ALU.subtract)
                    ins.then_inc(we_lo, 1)

                def turned(pair, h):
                    dve.wait_ge(xsT_hi, pair * HALVES + h + 1)
                    cols = slice(h * P, (h + 1) * P)
                    v.tensor_tensor(xsT[1][:, :, cols], psT[:, h, :].rearrange("p (k n) -> p k n", n=P),
                                    xsT[0][:, :, cols].bitcast(F32), ALU.subtract).then_inc(xsT_lo, 1)

                def product(pair, j):
                    rows = k_rows(j)
                    dve.wait_ge(gate_done, pair * KI + j + 1)
                    dve.wait_ge(hid_lo, pair * KI + j + 1)
                    v.tensor_tensor(hid[0:rows, j, :], psG[0:rows, j, 1, 0:PAIR], gate[0:rows, j, :], ALU.mult
                                    ).then_inc(hid_done, 1)

                def hidden(pair, j):
                    rows = k_rows(j)
                    dve.wait_ge(hid_hi, pair * KI + j + 1)
                    v.tensor_tensor(hidT[1][0:rows, j, :], hid[0:rows, j, :], hidT[0][0:rows, j, :].bitcast(F32),
                                    ALU.subtract).then_inc(hid_lo, 1)

                def tile_pair(pair, slot):
                    product(pair, 0)
                    for j in range(1, KI):
                        product(pair, j)
                        hidden(pair, j - 1)
                    hidden(pair, KI - 1)
                    for h in range(HALVES):
                        turned(pair + 1, h)

                for h in range(HALVES):
                    turned(0, h)
                experts(dve, split, tile_pair)

        experts_weights.close()

        stage = ExitStack()
        with stage:
            def sb(name, shape, dt=F32):
                return stage.enter_context(nc.sbuf_tensor(name, shape, dt))

            def sem(name):
                return stage.enter_context(nc.semaphore(name))

            wo = [sb(f"wo_{p}", [P, XT, H], F32R) for p in ("hi", "lo")]
            nw_col = sb("nw_col", [P, XT])
            xnrow = xnrow_c
            xT = [sb(f"c_xT_{p}", [P, KH, L], F32R) for p in ("hi", "lo")]
            gate = sb("c_gate", [P, 2, L])
            hid = sb("c_hid", [P, 2, L])
            hidT = [sb(f"c_hidT_{p}", [P, NJ, L], F32R) for p in ("hi", "lo")]
            y_raw = sb("y_raw", [P, C, XT * P])
            yT = [sb(f"yT_{p}", [P, XT * P], F32R) for p in ("hi", "lo")]
            ysq = sb("ysq_c", [P, XT * P])
            yred = sb("yred_c", [P, 2, P])
            nwt = sb("c_nwt", [P, 3, C])
            y_scale = sb("y_scale", [P, C])
            room = sb("room", [P, XT, H])
            picked_rows = [[room[:, 2 * i + k, :] for k in range(TOP)] for i in range(2)]
            moe = [room[:, 4 + i, :] for i in range(2)]
            xrow = [room[:, 6 + i, :] for i in range(2)]
            which = [[sb(f"c_which{i}{k}", [P, 1], U32) for k in range(TOP)] for i in range(2)]
            tick = sb("c_tick", [P, 1])
            nothing = sb("c_nothing", [P, 16])
            assert XT == 8 and TOP == 2
            psT = stage.enter_context(nc.psum_tensor("c_psT", [P, 512], F32))
            psG = stage.enter_context(nc.psum_tensor("c_psG", [P, 2, 2, 512], F32))
            psM = stage.enter_context(nc.psum_tensor("psM", [P, 2, 512], F32))
            psY = stage.enter_context(nc.psum_tensor("psY", [P, 512], F32))
            psQ = psY[:, :].rearrange("p (t l) -> p t l", l=P)

            assert NJ > C + 1
            first_turns = [psG[:, k // 2, k % 2, :] for k in range(KH)]

            nw_loaded = sem("nw_loaded")
            wo_loaded = sem("wo_loaded")
            wo_scaled = sem("wo_scaled")
            wo_hi = sem("wo_hi")
            wo_lo = sem("wo_lo")
            xn_loaded = sem("c_xn_loaded")
            x_loaded = [sem(f"c_x{i}_loaded") for i in range(2)]
            y_loaded = [sem(f"y{t}_loaded") for t in range(C)]
            rows_loaded = [[sem(f"rows{i}{k}_loaded") for k in range(TOP)] for i in range(2)]
            tick_made = sem("c_tick_made")
            which_done = sem("c_which_done")
            xT_full = sem("c_xT_full")
            xT_hi = sem("c_xT_hi")
            xT_lo = sem("c_xT_lo")
            gu_full = sem("c_gu_full")
            gate_done = sem("c_gate_done")
            hid_done = sem("c_hid_done")
            hid_hi = sem("c_hid_hi")
            hid_lo = sem("c_hid_lo")
            ysq_done = sem("ysq_done")
            yred_done = sem("yred_done")
            sq_full = sem("sq_full")
            sq_read = sem("sq_read")
            yT_hi = sem("yT_hi")
            yT_lo = sem("yT_lo")
            mix_full = sem("mix_full")
            moe_full = sem("moe_full")
            first_done = sem("first_done")
            moe_done = sem("moe_done")
            silu_done = sem("silu_done")
            mix_done = sem("mix_done")
            res_done = sem("res_done")
            res_stored = [sem(f"res{i}_stored") for i in range(2)]
            own = sem("c_own")
            block = stage.enter_context(nc.Block())
            OWN = 14

            def x_tile(dram, b, t):
                return dram.rearrange("b (c p) h -> b c p h", p=P)[b, t]

            @block.sync
            def _(sp):
                with nc.allow_non_contiguous_dma(reason="a small parameter"):
                    sp.dma_start(nw_col[:, :], norm_w.rearrange("(t p) -> p t", p=P)).then_inc(nw_loaded, 16)
                sp.dma_start(room[:, :, :], W_out.rearrange("(k p) n -> p k n", p=P)
                             ).then_inc(wo_loaded, 16)
                for t in range(C):
                    sp.dma_start(y_raw[:, t, :], y_dram[0, t]).then_inc(y_loaded[t], 16)
                sp.wait_ge(wo_lo, 1)
                for t in range(2):
                    sp.dma_start(xrow[t], x_tile(x, 0, t)).then_inc(x_loaded[t], 16)
                with sp.Fori(0, B) as b:
                    after_b = (b + 1) % B
                    sp.wait_ge(xT_full, b * KH + KH)
                    sp.dma_start(xnrow[:, :, :], xn_tok[after_b]).then_inc(xn_loaded, 16)
                    for t in range(C):
                        sp.wait_ge(yT_lo, b * C + t + 1)
                        sp.dma_start(y_raw[:, t, :], y_dram[after_b, t]).then_inc(y_loaded[t], 16)
                        sp.wait_ge(res_done, b * C + t + 3)
                        sp.dma_start(x_tile(out, b, t), xrow[t % 2]).then_inc(res_stored[t % 2], 16)
                        sp.wait_ge(res_stored[t % 2], b * 16 * (C // 2) + 16 * (t // 2) + 32)
                        if t + 2 < C:
                            src = x_tile(x, b, t + 2)
                        else:
                            src = x_tile(x, after_b, t + 2 - C)
                        sp.dma_start(xrow[t % 2], src).then_inc(x_loaded[t % 2], 16)
                for i in range(2):
                    sp.wait_ge(x_loaded[i], 16 * (B * C // 2 + 1))
                for t in range(C):
                    sp.wait_ge(y_loaded[t], 16 * (B + 1))
                sp.wait_ge(xn_loaded, 16 * B)

            @block.gpsimd
            def _(pool):
                g = nc.gpsimd
                g.memset(tick[:, :], 0.0).then_inc(tick_made, 1)
                pool.wait_ge(tick_made, 1)
                pool.wait_ge(wo_hi, 1)
                g.tensor_tensor(wo[1][:, :, :], room[:, :, :], wo[0][:, :, :].bitcast(F32),
                                ALU.subtract).then_inc(wo_lo, 1)
                pool.wait_ge(wo_lo, 1)
                with pool.Fori(0, NT // 2) as two:
                    for i in range(2):
                        n = two * 2 + i
                        pool.wait_ge(moe_done, n + 1)
                        for k in range(TOP):
                            g.tensor_copy(which[i][k][:, :], row_of[k][:, bass.ds(n, 1)]).then_inc(which_done, 1)
                        pool.wait_ge(which_done, n * TOP + TOP)
                        g.tensor_tensor(tick[:, :], tick[:, :], tick[:, :], ALU.add)
                        for k in range(TOP):
                            g.indirect_dma_start(out=picked_rows[i][k], out_offset=None,
                                                 in_=eo_dram[:, :],
                                                 in_offset=bass.IndirectOffsetOnAxis(ap=which[i][k][:, 0:1], axis=0)
                                                 ).then_inc(rows_loaded[i][k], 16)

            @block.tensor
            def _(pe):
                te = nc.tensor

                def turn(n, k):
                    pe.wait_ge(xT_lo, n + 1)
                    turn_into(psT[:, :], k)

                def turn_into(dst, k):
                    for c in range(C):
                        ins = te.transpose(dst[:, c * P:(c + 1) * P], xnrow[:, c, k * P:(k + 1) * P], ident[:, :])
                    ins.then_inc(xT_full, 1)

                for k in range(KH):
                    turn_into(first_turns[k], k)
                with pe.Fori(0, B) as b:
                    pe.wait_ge(xT_lo, b * KH + KH + 1)
                    for j in range(NJ):
                        pe.wait_ge(hid_done, b * NJ + j + 1)
                        for g in range(2 if j < SF else 1):
                            m = 0
                            for k in range(KH):
                                for a, c in PARTS:
                                    ins = te.matmul(psG[:, j % 2, g, :], ws[a][:, sw_cols(k, j, g)],
                                                    xT[c][:, k, :], start=(m == 0), stop=(m == 3 * KH - 1))
                                    m += 1
                        ins.then_inc(gu_full, 1)
                        if 1 <= j <= C:
                            t = j - 1
                            pe.wait_ge(yred_done, b * C + t + 2)
                            if t == 0:
                                pe.wait_ge(mix_done, b * C + 1)
                            te.matmul(psQ[:, t, :], yred[:, t % 2, :], ones[:, :], start=True, stop=True
                                      ).then_inc(sq_full, 1)
                    def mixer(t):
                        i = b * C + t
                        if t == 0:
                            pe.wait_ge(wo_lo, 1)
                            pe.wait_ge(sq_read, b + 1)
                        pe.wait_ge(yT_lo, i + 1)
                        pe.wait_ge(mix_done, i + 1)
                        m = 0
                        for k in range(XT):
                            for a, c in PARTS:
                                ins = te.matmul(psY[:, :], yT[a][:, k * P:(k + 1) * P], wo[c][:, k, :],
                                                start=(m == 0), stop=(m == 3 * XT - 1))
                                m += 1
                        ins.then_inc(mix_full, 1)

                    def down(t):
                        pe.wait_ge(first_done, b * C + t + 1)
                        m = 0
                        for j in range(NJ):
                            if t == 0:
                                pe.wait_ge(hid_lo, b * NJ + j + 3)
                            for a, c in PARTS:
                                ins = te.matmul(psM[:, t % 2, :], hidT[a][h_part(j), j, t * P:(t + 1) * P],
                                                ws[c][h_part(j), SGU + j * H:SGU + (j + 1) * H],
                                                start=(m == 0), stop=(m == 3 * NJ - 1))
                                m += 1
                        ins.then_inc(moe_full, 1)

                    mixer(0)
                    down(0)
                    for t in range(C):
                        if t:
                            down(t)
                        else:
                            pe.wait_ge(xn_loaded, b * 16 + 16)
                        turn(b * KH + KH + t, t)
                        if t:
                            mixer(t)

            @block.scalar
            def _(act):
                s = nc.scalar

                def turned(n, k, src=psT[:, :]):
                    act.wait_ge(xT_full, n + 1)
                    s.activation(xT[0][:, k, :], src, ACT.Copy).then_inc(xT_hi, 1)

                for k in range(KH):
                    turned(k, k, first_turns[k])

                act.wait_ge(wo_scaled, 1)
                s.activation(wo[0][:, :, :], room[:, :, :], ACT.Copy).then_inc(wo_hi, 1)

                with act.Fori(0, B) as b:
                    def silu(j):
                        act.wait_ge(gu_full, b * NJ + j + 1)
                        rows = P if j < SF else HALF
                        s.activation(gate[h_part(j), j % 2, :], psG[0:rows, j % 2, 0, :], ACT.Silu
                                     ).then_inc(gate_done, 1)

                    def hidden(j):
                        act.wait_ge(hid_done, b * NJ + j + 3)
                        s.activation(hidT[0][h_part(j), j, :], hid[h_part(j), j % 2, :], ACT.Copy).then_inc(hid_hi, 1)

                    def square(t):
                        act.wait_ge(y_loaded[t], b * 16 + 16)
                        act.wait_ge(yred_done, b * C + t + 1)
                        s.activation(ysq[:, :], y_raw[:, t, :], ACT.Square).then_inc(ysq_done, 1)

                    def split_y(t):
                        act.wait_ge(mix_full, b * C + t + 1)
                        s.activation(yT[0][:, :], y_raw[:, t, :], ACT.Copy).then_inc(yT_hi, 1)

                    for j in range(NJ):
                        if j < C:
                            square(j)
                        silu(j)
                        if j:
                            hidden(j - 1)
                        if j == C - 1:
                            split_y(0)
                    hidden(NJ - 1)
                    split_y(1)
                    for t in range(C):
                        turned(b * KH + KH + t, t)
                        act.wait_ge(moe_done, b * C + t + 3)
                        s.activation(moe[t % 2], moe[t % 2], ACT.Silu).then_inc(silu_done, 1)
                        if 0 < t < C - 1:
                            split_y(t + 1)

            @block.vector
            def _(dve):
                v = nc.vector
                for n, (sm, by) in enumerate(((xT_lo, 1), (hid_done, 2), (hid_lo, 2), (yred_done, 1), (sq_full, 2),
                                              (mix_full, 1), (first_done, 2), (moe_done, 2),
                                              (mix_done, 1), (res_done, 2), (res_stored[0], 16),
                                              (res_stored[1], 16))):
                    v.memset(nothing[:, n:n + 1], 0.0).then_inc(sm, by)

                def turned(n, k, src=psT[:, :]):
                    dve.wait_ge(xT_hi, n + 1)
                    v.tensor_tensor(xT[1][:, k, :], src, xT[0][:, k, :].bitcast(F32), ALU.subtract
                                    ).then_inc(xT_lo, 1)

                for k in range(KH):
                    turned(k, k, first_turns[k])
                dve.wait_ge(wo_loaded, 16)
                dve.wait_ge(nw_loaded, 16)
                for k in range(XT):
                    ins = v.tensor_scalar(room[:, k, :], room[:, k, :], nw_col[:, k:k + 1], None, ALU.mult)
                ins.then_inc(wo_scaled, 1)

                with dve.Fori(0, B) as b:
                    n_own = [0]

                    def then_read(ins):
                        n_own[0] += 1
                        ins.then_inc(own, 1)
                        dve.wait_ge(own, b * OWN + n_own[0])

                    def product(j):
                        part = h_part(j)
                        dve.wait_ge(gate_done, b * NJ + j + 1)
                        dve.wait_ge(hid_lo, b * NJ + j + 1)
                        v.tensor_tensor(hid[part, j % 2, :], psG[part, j % 2, int(j < SF), :], gate[part, j % 2, :],
                                        ALU.mult).then_inc(hid_done, 1)

                    def hidden(j):
                        part = h_part(j)
                        dve.wait_ge(hid_hi, b * NJ + j + 1)
                        v.tensor_tensor(hidT[1][part, j, :], hid[part, j % 2, :],
                                        hidT[0][part, j, :].bitcast(F32), ALU.subtract).then_inc(hid_lo, 1)

                    def reduce_squares(t):
                        dve.wait_ge(ysq_done, b * C + t + 1)
                        dve.wait_ge(sq_full, b * C + t + 1)
                        v.tensor_reduce(yred[:, t % 2, :], ysq[:, :].rearrange("p (j l) -> p l j", l=P), AX.X,
                                        ALU.add).then_inc(yred_done, 1)

                    def split_y(t):
                        dve.wait_ge(yT_hi, b * C + t + 1)
                        v.tensor_tensor(yT[1][:, :], y_raw[:, t, :], yT[0][:, :].bitcast(F32), ALU.subtract
                                        ).then_inc(yT_lo, 1)

                    v0, v1, v2 = (nwt[:, i, :] for i in range(3))
                    for j in range(NJ):
                        if j < C:
                            reduce_squares(j)
                        if j == C + 1:
                            dve.wait_ge(sq_full, b * C + C + 2)
                            v.tensor_scalar(v0, psQ[:, :, 0], 1.0 / INNER, 1e-5, ALU.mult, ALU.add
                                            ).then_inc(sq_read, 1)
                        product(j)
                        if j:
                            hidden(j - 1)
                        if j == C - 1:
                            split_y(0)
                    hidden(NJ - 1)
                    dve.wait_ge(sq_read, b + 1)
                    dve.wait_ge(mix_done, b * C + 1)
                    then_read(v.tensor_scalar(y_scale[:, :].bitcast(I32), v0.bitcast(I32), -0.5, 1597463007.0,
                                              ALU.mult, ALU.add))
                    for _ in range(4):
                        then_read(v.tensor_tensor(v1, y_scale[:, :], y_scale[:, :], ALU.mult))
                        then_read(v.scalar_tensor_tensor(out=v2, in0=v1, scalar=-0.5, in1=v0, op0=ALU.mult,
                                                         op1=ALU.mult))
                        then_read(v.scalar_tensor_tensor(out=y_scale[:, :], in0=v2, scalar=1.5, in1=y_scale[:, :],
                                                         op0=ALU.add, op1=ALU.mult))
                    for t in range(C):
                        i = b * C + t
                        if t == 0:
                            split_y(1)
                        half = b * 16 * (C // 2) + 16 * (t // 2) + 16
                        m = moe[t % 2]
                        dve.wait_ge(moe_full, i + 1)
                        dve.wait_ge(rows_loaded[t % 2][0], half)
                        dve.wait_ge(res_done, i + 1)
                        v.scalar_tensor_tensor(out=m, in0=picked_rows[t % 2][0],
                                               scalar=weight[0][:, bass.ds(i, 1)], in1=psM[:, t % 2, :],
                                               op0=ALU.mult, op1=ALU.add).then_inc(first_done, 1)
                        dve.wait_ge(first_done, i + 3)
                        dve.wait_ge(rows_loaded[t % 2][1], half)
                        v.scalar_tensor_tensor(out=m, in0=picked_rows[t % 2][1],
                                               scalar=weight[1][:, bass.ds(i, 1)], in1=m,
                                               op0=ALU.mult, op1=ALU.add).then_inc(moe_done, 1)
                        turned(b * KH + KH + t, t)
                        dve.wait_ge(silu_done, i + 1)
                        dve.wait_ge(mix_full, i + 2)
                        if t == 0:
                            then_read(v.memset(nothing[:, 15:16], 0.0))
                        v.scalar_tensor_tensor(out=m, in0=psY[:, :], scalar=y_scale[:, t:t + 1],
                                               in1=m, op0=ALU.mult, op1=ALU.mult).then_inc(mix_done, 1)
                        if 0 < t < C - 1:
                            split_y(t + 1)
                        dve.wait_ge(mix_done, i + 2)
                        dve.wait_ge(x_loaded[t % 2], half)
                        v.tensor_tensor(xrow[t % 2], m, xrow[t % 2], ALU.add).then_inc(res_done, 1)
                    assert n_own[0] == OWN, n_own[0]


_INPUTS = ["hidden_states", "W_in", "conv_w", "conv_b", "A", "D", "dt_bias", "norm_w", "W_out"]
_FFN = ["gate_w", "w_gate", "w_up", "w_down", "sw_gate", "sw_up", "sw_down"]


def kernel(**inputs):
    import numpy as np
    import concourse.bacc as bacc
    from concourse.bass_utils import run_bass_kernel_spmd

    names = ["L0_attn_" + n for n in _INPUTS] + ["L0_ffn_" + n for n in _FFN]
    nc = bacc.Bacc("TRN2", target_bir_lowering=False, num_devices=1)
    arrays, args = {}, []
    for name in names:
        a = np.ascontiguousarray(inputs[name])
        arrays[name + "_dram"] = a
        args.append(nc.dram_tensor(name + "_dram", a.shape, mybir.dt.from_np(a.dtype), kind="ExternalInput").ap())
    out = nc.dram_tensor("out_dram", inputs["L0_attn_hidden_states"].shape, F32, kind="ExternalOutput").ap()
    program(nc, *args, out)
    result = run_bass_kernel_spmd(nc, [arrays], core_ids=[0])
    return result.results[0]["out_dram"]
```
